# Optimizing a Trainium2 kernel written in Bass

```python
import numpy as np
import jax
import jax.numpy as jnp

def _softmax(x, axis=-1):
    return jax.nn.softmax(x, axis=axis)

def _gelu(x):
    return jax.nn.gelu(x, approximate=True)

def _silu(x):
    return jax.nn.silu(x)

def _sigmoid(x):
    return jax.nn.sigmoid(x)

def _layernorm(x, axis=-1, eps=1e-05):
    m = jnp.mean(x, axis=axis, keepdims=True)
    v = jnp.var(x, axis=axis, keepdims=True)
    return (x - m) / jnp.sqrt(v + eps)

def _scatter_add(tgt, idx, src, axis=0):
    return tgt.at[idx].add(src)

def _segment_sum(src, seg, n):
    return jax.ops.segment_sum(src, seg, n)
kernel_name = 'mk_perceiver_d2_seqx_r4_c92b39'

def setup_inputs(seed: int=0):
    np.random.seed(seed)
    _w = jnp.asarray

    def _rec_inputs():
        import jax
        import jax.numpy as jnp
        _rk = jax.random.key(seed)
        x = -0.0002928 + 1 * jax.random.normal(jax.random.fold_in(_rk, 1), (64, 64, 256), jnp.float32)
        _lenS = 64 - jax.random.randint(jax.random.fold_in(_rk, 7), (64,), 0, max(1, 64 // 4) + 1, jnp.int32)
        _lenS2 = 256 - jax.random.randint(jax.random.fold_in(_rk, 8), (64,), 0, max(1, 256 // 4) + 1, jnp.int32)
        _ctx_1024P = jax.random.normal(jax.random.fold_in(_rk, 11), (64, 16, 256), jnp.float32)
        _ctx_1024c = jax.random.dirichlet(jax.random.fold_in(_rk, 511), 0.3 * jnp.ones((16,), jnp.float32), (64, 256))
        _ctx_1024t = jnp.einsum('bsk,bkd->bsd', _ctx_1024c, _ctx_1024P)
        _ctx_1024t = _ctx_1024t * jax.lax.rsqrt(jnp.mean(jnp.square(_ctx_1024t)) + 1e-12) * 0.953939
        ctx_1024 = -1.39393e-06 + 0.999914 * (_ctx_1024t + 0.3 * jax.random.normal(jax.random.fold_in(_rk, 611), (64, 256, 256), jnp.float32))
        _validS = jnp.arange(64)[None, :] < _lenS[:, None]
        _validS2 = jnp.arange(256)[None, :] < _lenS2[:, None]
        _causal = jnp.tril(jnp.ones((64, 64), dtype=bool))
        mask_Bx1xSxS2_ik1 = jnp.where(jnp.broadcast_to(_validS2[:, None, None, :], (64, 1, 64, 256)), 1, 0).astype(jnp.int32)
        return (x, ctx_1024, mask_Bx1xSxS2_ik1)
    x, ctx_1024, mask_Bx1xSxS2_ik1 = _rec_inputs()

    def _L0_xattn_setup():
        import jax, jax.numpy as jnp
        import numpy as np
        HEADS = 16
        DIM_HEAD = 64
        QUERY_DIM = 256
        INNER = HEADS * DIM_HEAD
        SCALE = DIM_HEAD ** (-0.5)
        key = jax.random.key(seed)
        ks = jax.random.split(key, 6)
        B, N, M = (2, 512, 512)
        x = jax.random.normal(ks[0], (B, N, QUERY_DIM), dtype=jnp.float32)
        context = jax.random.normal(ks[1], (B, M, QUERY_DIM), dtype=jnp.float32)
        s = QUERY_DIM ** (-0.5)
        Wq = jax.random.normal(ks[2], (QUERY_DIM, INNER), dtype=jnp.float32) * s
        Wk = jax.random.normal(ks[3], (QUERY_DIM, INNER), dtype=jnp.float32) * s
        Wv = jax.random.normal(ks[4], (QUERY_DIM, INNER), dtype=jnp.float32) * s
        Wo = jax.random.normal(ks[5], (INNER, QUERY_DIM), dtype=jnp.float32) * INNER ** (-0.5)
        return {'x': x, 'context': context, 'Wq': Wq, 'Wk': Wk, 'Wv': Wv, 'Wo': Wo}
    _L0_xattn_all = _L0_xattn_setup()
    _L0_xattn_in = {k: v for k, v in _L0_xattn_all.items() if k in ('Wq', 'Wk', 'Wv', 'Wo')}
    del _L0_xattn_all

    def _L0_attn_setup():
        import jax, jax.numpy as jnp
        import numpy as np
        NUM_HEADS = 16
        D_MODEL = 256
        DEPTH = D_MODEL // NUM_HEADS

        def rope_sincos(seq_len, depth):
            inv_freq = 1.0 / 10000.0 ** (jnp.arange(0, depth, 2, dtype=jnp.float32) / depth)
            ang = jnp.arange(seq_len, dtype=jnp.float32)[:, None] * inv_freq[None, :]
            sin = jnp.concatenate([jnp.sin(ang), jnp.sin(ang)], axis=-1)
            cos = jnp.concatenate([jnp.cos(ang), jnp.cos(ang)], axis=-1)
            return (sin, cos)

        def apply_rope(x, sin, cos):
            half = x.shape[-1] // 2
            x1, x2 = (x[..., :half], x[..., half:])
            rot = jnp.concatenate([-x2, x1], axis=-1)
            return x * cos + rot * sin
        key = jax.random.key(seed)
        ks = jax.random.split(key, 5)
        s = 1.0 / np.sqrt(D_MODEL)
        return {'x': jax.random.normal(ks[0], (2, 512, D_MODEL), dtype=jnp.float32), 'wq': jax.random.normal(ks[1], (D_MODEL, D_MODEL), dtype=jnp.float32) * s, 'bq': jnp.zeros((D_MODEL,), jnp.float32), 'wk': jax.random.normal(ks[2], (D_MODEL, D_MODEL), dtype=jnp.float32) * s, 'bk': jnp.zeros((D_MODEL,), jnp.float32), 'wv': jax.random.normal(ks[3], (D_MODEL, D_MODEL), dtype=jnp.float32) * s, 'bv': jnp.zeros((D_MODEL,), jnp.float32), 'wo': jax.random.normal(ks[4], (D_MODEL, D_MODEL), dtype=jnp.float32) * s, 'bo': jnp.zeros((D_MODEL,), jnp.float32)}
    _L0_attn_all = _L0_attn_setup()
    _L0_attn_in = {k: v for k, v in _L0_attn_all.items() if k in ('wq', 'bq', 'wk', 'bk', 'wv', 'bv', 'wo', 'bo')}
    del _L0_attn_all

    def _L0_ffn_setup():
        import jax, jax.numpy as jnp
        import numpy as np
        EPS_NORM = 1e-08
        EPS_Q = 1e-05

        def rmsnorm(x, w):
            v = jnp.mean(jnp.square(x.astype(jnp.float32)), axis=-1, keepdims=True)
            x_hat = x * jax.lax.rsqrt(v + EPS_NORM)
            return (x_hat * w).astype(x.dtype)

        def activation_quant(x):
            scale = 127.0 / jnp.clip(jnp.max(jnp.abs(x), axis=-1, keepdims=True), EPS_Q, None)
            return jnp.clip(jnp.round(x * scale), -128, 127) / scale

        def weight_quant(w):
            scale = 1.0 / jnp.clip(jnp.mean(jnp.abs(w)), EPS_Q, None)
            return jnp.clip(jnp.round(w * scale), -1, 1) / scale

        def bitlinear(x, norm_w, w):
            x_norm = rmsnorm(x, norm_w)
            x_q = x_norm + jax.lax.stop_gradient(activation_quant(x_norm) - x_norm)
            w_q = w + jax.lax.stop_gradient(weight_quant(w) - w)
            return jnp.einsum('bsd,hd->bsh', x_q, w_q)
        key = jax.random.key(seed)
        k1, k2, k3 = jax.random.split(key, 3)
        dim, hidden = (256, 1024)
        return {'x': jax.random.normal(k1, (4, 512, dim), dtype=jnp.float32), 'norm1_w': jnp.ones((dim,), jnp.float32), 'w1': jax.random.normal(k2, (hidden, dim), jnp.float32) * 0.02, 'act_scale': jnp.ones((1,), jnp.float32), 'act_bias': jnp.zeros((1,), jnp.float32), 'norm2_w': jnp.ones((hidden,), jnp.float32), 'w2': jax.random.normal(k3, (dim, hidden), jnp.float32) * 0.02}
    _L0_ffn_all = _L0_ffn_setup()
    _L0_ffn_in = {k: v for k, v in _L0_ffn_all.items() if k in ('norm1_w', 'w1', 'act_scale', 'act_bias', 'norm2_w', 'w2')}
    del _L0_ffn_all

    def _L1_xattn_setup():
        import jax, jax.numpy as jnp
        import numpy as np
        EMBED = 256
        HEADS = 16
        HEAD_DIM = EMBED // HEADS
        B, S = (4, 512)
        key = jax.random.key(seed)
        ks = jax.random.split(key, 9)
        inp = {'values': jax.random.normal(ks[0], (B, S, EMBED), jnp.float32), 'keys': jax.random.normal(ks[1], (B, S, EMBED), jnp.float32), 'queries': jax.random.normal(ks[2], (B, S, EMBED), jnp.float32), 'mask': jax.random.randint(ks[3], (B, 1, S, S), 0, 2, jnp.int32), 'Wv': jax.random.normal(ks[4], (HEAD_DIM, HEAD_DIM), jnp.float32) / np.sqrt(HEAD_DIM), 'Wk': jax.random.normal(ks[5], (HEAD_DIM, HEAD_DIM), jnp.float32) / np.sqrt(HEAD_DIM), 'Wq': jax.random.normal(ks[6], (HEAD_DIM, HEAD_DIM), jnp.float32) / np.sqrt(HEAD_DIM), 'Wo': jax.random.normal(ks[7], (EMBED, EMBED), jnp.float32) / np.sqrt(EMBED), 'bo': jax.random.normal(ks[8], (EMBED,), jnp.float32) * 0.01}
        return inp
    _L1_xattn_all = _L1_xattn_setup()
    _L1_xattn_in = {k: v for k, v in _L1_xattn_all.items() if k in ('Wv', 'Wk', 'Wq', 'Wo', 'bo')}
    del _L1_xattn_all

    def _L1_attn_setup():
        import jax, jax.numpy as jnp
        import numpy as np
        D_MODEL = 256
        N_HEADS = 16
        HEAD_DIM = D_MODEL // N_HEADS
        BATCH = 2
        SEQ = 512

        def _alibi_bias(seq_len, n_heads, dtype):
            slopes = 1.0 / 2.0 ** (jnp.arange(n_heads, dtype=dtype) / n_heads)
            rel = jnp.arange(seq_len, dtype=dtype)[None, :] - jnp.arange(seq_len, dtype=dtype)[:, None]
            return slopes[:, None, None] * rel[None, :, :]
        key = jax.random.key(seed)
        ks = jax.random.split(key, 9)
        s = 0.02
        return {'x': jax.random.normal(ks[0], (BATCH, SEQ, D_MODEL), dtype=jnp.float32), 'Wq': jax.random.normal(ks[1], (D_MODEL, D_MODEL), dtype=jnp.float32) * s, 'bq': jnp.zeros((D_MODEL,), dtype=jnp.float32), 'Wk': jax.random.normal(ks[2], (D_MODEL, D_MODEL), dtype=jnp.float32) * s, 'bk': jnp.zeros((D_MODEL,), dtype=jnp.float32), 'Wv': jax.random.normal(ks[3], (D_MODEL, D_MODEL), dtype=jnp.float32) * s, 'bv': jnp.zeros((D_MODEL,), dtype=jnp.float32), 'Wo': jax.random.normal(ks[4], (D_MODEL, D_MODEL), dtype=jnp.float32) * s, 'bo': jnpp_zeros() if False else jnp.zeros((D_MODEL,), dtype=jnp.float32)}
    _L1_attn_all = _L1_attn_setup()
    _L1_attn_in = {k: v for k, v in _L1_attn_all.items() if k in ('Wq', 'bq', 'Wk', 'bk', 'Wv', 'bv', 'Wo', 'bo')}
    del _L1_attn_all

    def _L1_ffn_setup():
        import jax, jax.numpy as jnp
        import numpy as np
        D = 256
        I = 128
        E = 32
        K = 4
        T = 2 * 512
        C = 2 * T * K // E
        key = jax.random.key(seed)
        ks = jax.random.split(key, 9)
        bf = jnp.bfloat16
        std = 0.02
        x = jax.random.normal(ks[0], (2, 512, D), dtype=jnp.float32).astype(bf)
        gate_w = (std * jax.random.normal(ks[1], (E, D), dtype=jnp.float32)).astype(bf)
        bias = jnp.zeros((E,), jnp.float32)
        W1 = (std * jax.random.normal(ks[2], (E, D, I), dtype=jnp.float32)).astype(bf)
        W3 = (std * jax.random.normal(ks[3], (E, D, I), dtype=jnp.float32)).astype(bf)
        W2 = (std * jax.random.normal(ks[4], (E, I, D), dtype=jnp.float32)).astype(bf)
        sw1 = (std * jax.random.normal(ks[5], (I, D), dtype=jnp.float32)).astype(bf)
        sw3 = (std * jax.random.normal(ks[6], (I, D), dtype=jnp.float32)).astype(bf)
        sw2 = (std * jax.random.normal(ks[7], (D, I), dtype=jnp.float32)).astype(bf)
        return {'x': x, 'gate_w': gate_w, 'bias': bias, 'W1': W1, 'W3': W3, 'W2': W2, 'sw1': sw1, 'sw3': sw3, 'sw2': sw2}
    _L1_ffn_all = _L1_ffn_setup()
    _L1_ffn_in = {k: v for k, v in _L1_ffn_all.items() if k in ('gate_w', 'bias', 'W1', 'W3', 'W2', 'sw1', 'sw3', 'sw2')}
    del _L1_ffn_all
    return {'x': x, 'ctx_1024': ctx_1024, 'mask_Bx1xSxS2_ik1': mask_Bx1xSxS2_ik1, 'L0_xattn_Wq': _L0_xattn_in['Wq'], 'L0_xattn_Wk': _L0_xattn_in['Wk'], 'L0_xattn_Wv': _L0_xattn_in['Wv'], 'L0_xattn_Wo': _L0_xattn_in['Wo'], 'L0_attn_wq': _L0_attn_in['wq'], 'L0_attn_bq': _L0_attn_in['bq'], 'L0_attn_wk': _L0_attn_in['wk'], 'L0_attn_bk': _L0_attn_in['bk'], 'L0_attn_wv': _L0_attn_in['wv'], 'L0_attn_bv': _L0_attn_in['bv'], 'L0_attn_wo': _L0_attn_in['wo'], 'L0_attn_bo': _L0_attn_in['bo'], 'L0_ffn_norm1_w': _L0_ffn_in['norm1_w'], 'L0_ffn_w1': _L0_ffn_in['w1'], 'L0_ffn_act_scale': _L0_ffn_in['act_scale'], 'L0_ffn_act_bias': _L0_ffn_in['act_bias'], 'L0_ffn_norm2_w': _L0_ffn_in['norm2_w'], 'L0_ffn_w2': _L0_ffn_in['w2'], 'L1_xattn_Wv': _L1_xattn_in['Wv'], 'L1_xattn_Wk': _L1_xattn_in['Wk'], 'L1_xattn_Wq': _L1_xattn_in['Wq'], 'L1_xattn_Wo': _L1_xattn_in['Wo'], 'L1_xattn_bo': _L1_xattn_in['bo'], 'L1_attn_Wq': _L1_attn_in['Wq'], 'L1_attn_bq': _L1_attn_in['bq'], 'L1_attn_Wk': _L1_attn_in['Wk'], 'L1_attn_bk': _L1_attn_in['bk'], 'L1_attn_Wv': _L1_attn_in['Wv'], 'L1_attn_bv': _L1_attn_in['bv'], 'L1_attn_Wo': _L1_attn_in['Wo'], 'L1_attn_bo': _L1_attn_in['bo'], 'L1_ffn_gate_w': _L1_ffn_in['gate_w'], 'L1_ffn_bias': _L1_ffn_in['bias'], 'L1_ffn_W1': _L1_ffn_in['W1'], 'L1_ffn_W3': _L1_ffn_in['W3'], 'L1_ffn_W2': _L1_ffn_in['W2'], 'L1_ffn_sw1': _L1_ffn_in['sw1'], 'L1_ffn_sw3': _L1_ffn_in['sw3'], 'L1_ffn_sw2': _L1_ffn_in['sw2']}

def reference(x, ctx_1024, mask_Bx1xSxS2_ik1, L0_xattn_Wq, L0_xattn_Wk, L0_xattn_Wv, L0_xattn_Wo, L0_attn_wq, L0_attn_bq, L0_attn_wk, L0_attn_bk, L0_attn_wv, L0_attn_bv, L0_attn_wo, L0_attn_bo, L0_ffn_norm1_w, L0_ffn_w1, L0_ffn_act_scale, L0_ffn_act_bias, L0_ffn_norm2_w, L0_ffn_w2, L1_xattn_Wv, L1_xattn_Wk, L1_xattn_Wq, L1_xattn_Wo, L1_xattn_bo, L1_attn_Wq, L1_attn_bq, L1_attn_Wk, L1_attn_bk, L1_attn_Wv, L1_attn_bv, L1_attn_Wo, L1_attn_bo, L1_ffn_gate_w, L1_ffn_bias, L1_ffn_W1, L1_ffn_W3, L1_ffn_W2, L1_ffn_sw1, L1_ffn_sw3, L1_ffn_sw2):
    import jax
    import jax.numpy as jnp

    def _L0_xattn_ref(x, context, Wq, Wk, Wv, Wo):
        import jax, jax.numpy as jnp
        import numpy as np
        HEADS = 16
        DIM_HEAD = 64
        QUERY_DIM = 256
        INNER = HEADS * DIM_HEAD
        SCALE = DIM_HEAD ** (-0.5)
        B, N, _ = x.shape
        M = context.shape[1]
        q = (x @ Wq).reshape(B, N, HEADS, DIM_HEAD)
        k = (context @ Wk).reshape(B, M, HEADS, DIM_HEAD)
        v = (context @ Wv).reshape(B, M, HEADS, DIM_HEAD)
        sim = jnp.einsum('bihd,bjhd->bhij', q, k) * SCALE
        attn = jax.nn.softmax(sim, axis=-1)
        out = jnp.einsum('bhij,bjhd->bihd', attn, v)
        out = out.reshape(B, N, INNER)
        return out @ Wo

    def _L0_attn_ref(x, wq, bq, wk, bk, wv, bv, wo, bo):
        import jax, jax.numpy as jnp
        import numpy as np
        NUM_HEADS = 16
        D_MODEL = 256
        DEPTH = D_MODEL // NUM_HEADS

        def rope_sincos(seq_len, depth):
            inv_freq = 1.0 / 10000.0 ** (jnp.arange(0, depth, 2, dtype=jnp.float32) / depth)
            ang = jnp.arange(seq_len, dtype=jnp.float32)[:, None] * inv_freq[None, :]
            sin = jnp.concatenate([jnp.sin(ang), jnp.sin(ang)], axis=-1)
            cos = jnp.concatenate([jnp.cos(ang), jnp.cos(ang)], axis=-1)
            return (sin, cos)

        def apply_rope(x, sin, cos):
            half = x.shape[-1] // 2
            x1, x2 = (x[..., :half], x[..., half:])
            rot = jnp.concatenate([-x2, x1], axis=-1)
            return x * cos + rot * sin
        B, S, _ = x.shape

        def split_heads(t):
            return t.reshape(B, S, NUM_HEADS, DEPTH).transpose(0, 2, 1, 3)
        Q = split_heads(x @ wq + bq)
        K = split_heads(x @ wk + bk)
        V = split_heads(x @ wv + bv)
        sin, cos = rope_sincos(S, DEPTH)
        Q = apply_rope(Q, sin, cos)
        K = apply_rope(K, sin, cos)
        scores = jnp.einsum('bhqd,bhkd->bhqk', Q, K) / jnp.sqrt(jnp.float32(DEPTH))
        weights = jax.nn.softmax(scores, axis=-1)
        out = jnp.einsum('bhqk,bhkd->bhqd', weights, V)
        out = out.transpose(0, 2, 1, 3).reshape(B, S, D_MODEL)
        return out @ wo + bo

    def _L0_ffn_ref(x, norm1_w, w1, act_scale, act_bias, norm2_w, w2):
        import jax, jax.numpy as jnp
        import numpy as np
        EPS_NORM = 1e-08
        EPS_Q = 1e-05

        def rmsnorm(x, w):
            v = jnp.mean(jnp.square(x.astype(jnp.float32)), axis=-1, keepdims=True)
            x_hat = x * jax.lax.rsqrt(v + EPS_NORM)
            return (x_hat * w).astype(x.dtype)

        def activation_quant(x):
            scale = 127.0 / jnp.clip(jnp.max(jnp.abs(x), axis=-1, keepdims=True), EPS_Q, None)
            return jnp.clip(jnp.round(x * scale), -128, 127) / scale

        def weight_quant(w):
            scale = 1.0 / jnp.clip(jnp.mean(jnp.abs(w)), EPS_Q, None)
            return jnp.clip(jnp.round(w * scale), -1, 1) / scale

        def bitlinear(x, norm_w, w):
            x_norm = rmsnorm(x, norm_w)
            x_q = x_norm + jax.lax.stop_gradient(activation_quant(x_norm) - x_norm)
            w_q = w + jax.lax.stop_gradient(weight_quant(w) - w)
            return jnp.einsum('bsd,hd->bsh', x_q, w_q)
        h = bitlinear(x, norm1_w, w1)
        h = act_scale * jnp.square(jax.nn.relu(h)) + act_bias
        y = bitlinear(h, norm2_w, w2)
        return y

    def _L1_xattn_ref(values, keys, queries, mask, Wv, Wk, Wq, Wo, bo):
        import jax, jax.numpy as jnp
        import numpy as np
        EMBED = 256
        HEADS = 16
        HEAD_DIM = EMBED // HEADS
        B, S = (4, 512)
        N, q_len = (queries.shape[0], queries.shape[1])
        v_len, k_len = (values.shape[1], keys.shape[1])
        v = values.reshape(N, v_len, HEADS, HEAD_DIM)
        k = keys.reshape(N, k_len, HEADS, HEAD_DIM)
        q = queries.reshape(N, q_len, HEADS, HEAD_DIM)
        v = jnp.einsum('nlhd,ed->nlhe', v, Wv)
        k = jnp.einsum('nlhd,ed->nlhe', k, Wk)
        q = jnp.einsum('nlhd,ed->nlhe', q, Wq)
        energy = jnp.einsum('nqhd,nkhd->nhqk', q, k)
        energy = jnp.where(mask == 0, jnp.float32(-1e+20), energy)
        attention = jax.nn.softmax(energy / np.sqrt(EMBED).astype(np.float32), axis=3)
        out = jnp.einsum('nhql,nlhd->nqhd', attention, v).reshape(N, q_len, EMBED)
        return out @ Wo.T + bo

    def _L1_attn_ref(x, Wq, bq, Wk, bk, Wv, bv, Wo, bo):
        import jax, jax.numpy as jnp
        import numpy as np
        D_MODEL = 256
        N_HEADS = 16
        HEAD_DIM = D_MODEL // N_HEADS
        BATCH = 2
        SEQ = 512

        def _alibi_bias(seq_len, n_heads, dtype):
            slopes = 1.0 / 2.0 ** (jnp.arange(n_heads, dtype=dtype) / n_heads)
            rel = jnp.arange(seq_len, dtype=dtype)[None, :] - jnp.arange(seq_len, dtype=dtype)[:, None]
            return slopes[:, None, None] * rel[None, :, :]
        B, S, D = x.shape
        H, Hd = (N_HEADS, HEAD_DIM)
        scale = Hd ** (-0.5)
        Q = (x @ Wq + bq).reshape(B, S, H, Hd)
        K = (x @ Wk + bk).reshape(B, S, H, Hd)
        V = (x @ Wv + bv).reshape(B, S, H, Hd)
        scores = jnp.einsum('bqhd,bkhd->bhqk', Q, K) * scale
        scores = scores + _alibi_bias(S, H, x.dtype)[None]
        attn = jax.nn.softmax(scores, axis=-1)
        out = jnp.einsum('bhqk,bkhd->bqhd', attn, V).reshape(B, S, D)
        return out @ Wo + bo

    def _L1_ffn_ref(x, gate_w, bias, W1, W3, W2, sw1, sw3, sw2):
        import jax, jax.numpy as jnp
        import numpy as np
        D = 256
        I = 128
        E = 32
        K = 4
        T = 2 * 512
        C = 2 * T * K // E
        X = x.reshape(-1, D)
        logits = (X @ gate_w.T).astype(jnp.float32)
        scores = jax.nn.sigmoid(logits)
        _, idx = jax.lax.top_k(scores + bias[None, :], K)
        w = jnp.take_along_axis(scores, idx, axis=-1)
        w = w / jnp.clip(jnp.sum(w, axis=-1, keepdims=True), 1e-12, None)
        w = w.astype(x.dtype)
        eid = idx.reshape(-1)
        onehot = (eid[:, None] == jnp.arange(E)[None, :]).astype(jnp.int32)
        pos = jnp.take_along_axis(jnp.cumsum(onehot, axis=0) - 1, eid[:, None], axis=1)[:, 0]
        valid = pos < C
        posc = jnp.minimum(pos, C - 1)
        Xrep = jnp.repeat(X, K, axis=0)
        xe = jnp.zeros((E, C, D), x.dtype).at[eid, posc].add(jnp.where(valid[:, None], Xrep, jnp.zeros((), x.dtype)))
        h = jax.nn.silu(jnp.einsum('ecd,edi->eci', xe, W1)) * jnp.einsum('ecd,edi->eci', xe, W3)
        ye = jnp.einsum('eci,eid->ecd', h, W2)
        gflat = jnp.where(valid, w.reshape(-1), jnp.zeros((), x.dtype))
        yrows = ye[eid, posc] * gflat[:, None]
        out = yrows.reshape(-1, K, D).sum(axis=1)
        out = out + jax.nn.silu(X @ sw1.T) * (X @ sw3.T) @ sw2.T
        return out.reshape(x.shape)
    x = x + _L0_xattn_ref(_layernorm(x, axis=-1), ctx_1024, L0_xattn_Wq, L0_xattn_Wk, L0_xattn_Wv, L0_xattn_Wo)
    x = x + _L0_attn_ref(_layernorm(x, axis=-1), L0_attn_wq, L0_attn_bq, L0_attn_wk, L0_attn_bk, L0_attn_wv, L0_attn_bv, L0_attn_wo, L0_attn_bo)
    x = x + _L0_ffn_ref(_layernorm(x, axis=-1), L0_ffn_norm1_w, L0_ffn_w1, L0_ffn_act_scale, L0_ffn_act_bias, L0_ffn_norm2_w, L0_ffn_w2)
    x = x + _L1_xattn_ref(ctx_1024, ctx_1024, _layernorm(x, axis=-1), mask_Bx1xSxS2_ik1, L1_xattn_Wv, L1_xattn_Wk, L1_xattn_Wq, L1_xattn_Wo, L1_xattn_bo)
    x = x + _L1_attn_ref(_layernorm(x, axis=-1), L1_attn_Wq, L1_attn_bq, L1_attn_Wk, L1_attn_bk, L1_attn_Wv, L1_attn_bv, L1_attn_Wo, L1_attn_bo)
    x = x + _L1_ffn_ref(_layernorm(x, axis=-1), L1_ffn_gate_w, L1_ffn_bias, L1_ffn_W1, L1_ffn_W3, L1_ffn_W2, L1_ffn_sw1, L1_ffn_sw3, L1_ffn_sw2)
    return x

_drawn_inputs = setup_inputs


def setup_inputs(seed=0):
    import zlib

    import numpy as np

    out = dict(_drawn_inputs(seed))
    spreads = {'L0_attn_bq': (0.0, 0.607),
     'L0_attn_bk': (0.0, 0.799),
     'L0_attn_bv': (0.0, 0.1),
     'L0_attn_bo': (0.0, 0.1),
     'L0_ffn_norm1_w': (1.0, 0.2),
     'L0_ffn_norm2_w': (1.0, 0.2),
     'L1_attn_bq': (0.0, 0.8),
     'L1_attn_bk': (0.0, 0.8),
     'L1_attn_bv': (0.0, 0.328),
     'L1_attn_bo': (0.0, 0.1),
     'L1_ffn_bias': (0.0, 0.8)}
    factors = {'L1_xattn_bo': 8.0,
     'L1_attn_Wq': 8.0,
     'L1_attn_Wk': 8.0,
     'L1_ffn_gate_w': 8.0,
     'L1_ffn_W1': 8.0,
     'L1_ffn_W3': 8.0,
     'L1_ffn_W2': 8.0,
     'L1_ffn_sw1': 6.822,
     'L1_ffn_sw3': 6.696,
     'L1_ffn_sw2': 6.71}
    for name, (base, spread) in spreads.items():
        noise = np.random.default_rng([zlib.crc32(name.encode()), seed]).standard_normal(out[name].shape)
        drawn = base * np.exp(spread * noise) if base else spread * noise
        out[name] = jnp.asarray(drawn.astype(out[name].dtype))
    for name, factor in factors.items():
        out[name] = (out[name] * factor).astype(out[name].dtype)
    return out
```

```python
from contextlib import ExitStack

import numpy as np

import concourse.bass as bass
from concourse import mybir

F32 = mybir.dt.float32
BF16 = mybir.dt.bfloat16
I32 = mybir.dt.int32
U32 = mybir.dt.uint32
ALU = mybir.AluOpType
ACT = mybir.ActivationFunctionType
AX = mybir.AxisListType

P = 128
S = 64
D = 256
DC = D // P
CTX = 256
KC = CTX // P
H = 16
PAIRS = H // 2
DH = 64
HD = D // H
FF = 1024
E = 32
TOPK = 4
EI = 128
CAP = 2 * (2 * 512) * TOPK // E
EPS = 1e-5
MAGIC = 12582912.0
FAR = float(1 << 20)
UNITS = 8


class Tile:

    def __init__(self, c, i=None):
        self.c, self.i = c, i
        self.par = c % 2

    def back(self, n):
        return Tile(self.c - n, self.i)

    @property
    def exists(self):
        return self.i is not None or self.c >= 0

    def count(self, per_tile, k):
        v = self.c * per_tile + k
        return v if self.i is None else self.i * (2 * per_tile) + v

    def loads(self):
        v = 16 * (self.c // 2 + 1)
        return v if self.i is None else self.i * 16 + v

    def landed(self, n):
        return self.loads() * n if self.i is None else self.i * (16 * n) + 16 * n * (self.c // 2 + 1)

    def row(self):
        return self.c if self.i is None else self.i * 2 + self.c


class Chain:

    def __init__(self, sem, steps):
        self.sem, self.index, n = sem, {}, 0
        for step in steps:
            name, k = step if isinstance(step, tuple) else (step, 1)
            assert name not in self.index, name
            n += k
            self.index[name] = n
        self.per_tile = n

    def at(self, tile, step):
        return tile.count(self.per_tile, self.index[step])


class Signal:

    def __init__(self, sem, per_tile):
        self.sem, self.per_tile = sem, per_tile

    def at(self, tile, k):
        return tile.count(self.per_tile, k + 1)


def after(eng, source, tile, step):
    if tile.exists:
        eng.wait_ge(source.sem, source.at(tile, step))


NORM = ["stats", "mean", "var", "rstd", "xn", "xnT_ps", "xnT"]
QKV_A = [("qT_ps", 1), ("qT", 2)] + [x for n in range(4) for x in (f"qk_ps{n}", (f"qk{n}", 2))]
SOFTMAX = ["shifted", "exp", "pT_ps", ("pT", 2), "out_ps", ("heads", 4),
           "headsT_ps", "headsT", "proj_ps", "added", "biased"]
ROPE_ATTN = NORM + ["qkv_ps", ("qkv", 2), ("turned", 3), "roped", "qkT_ps", ("qkT", 5),
                    "scores_ps", "max"] + SOFTMAX
QUANT = ["var", "rstd", "peak", "guarded", "inverse", "factor", "undo", "clipped", "rounded", "quant"]
FFN = (NORM[:5] + [("weighed", 2)] + ["in_" + x for x in QUANT] + ["inT_ps", "inT", "up_ps", ("relu", 2), "square",
       "affine", ("weighed2", 2)] + ["mid_" + x for x in QUANT] + ["midT_ps", "midT", "down_ps", "added"])
MASKED = (NORM + ["q_ps", ("q", 4)]
          + [(f"{name}{u}", k) for u in range(4) for name, k in
             (("scores_ps", 1), ("masked", 4), ("offset", 1), ("exp", 4), ("pT_ps", 1), ("pT", 2),
              ("out_ps", 1), ("heads", 2))]
          + ["headsT_ps", "headsT", "proj_ps", "added", "biased"])
ALIBI_ATTN = NORM + ["qkv_ps", ("qkv", 11), "scores_ps", ("alibi", 2), "max"] + SOFTMAX
ROUTE = (NORM + ["up_ps", ("exp", 2), ("plus1", 2), ("inverse", 2), ("scores", 2), ("top", 2), "index", "index_f",
                 ("hot", 4), ("chosen", 2), "weight", "total", "guarded", "over_total", "gates", "pos_ps",
                 ("hot_pos", 2), "pos", ("limits", 5), ("places", 3), "put"])

A_STAGES = (["a_ln", "a_xt", "a_q"] + [("a_qp", c, g) for c in range(DC) for g in range(2)]
            + [("a_s", 0), ("a_s", 1)]
            + [x for u in range(UNITS)
               for x in ([("a_tr", u)] + ([("a_s", u + 2)] if u + 2 < UNITS else []) + [("a_z", u)])]
            + ["a_v", "a_y"])
B_STAGES = (["b_ln", "b_xt", "b_qkv", "b_qkt", "b_s", "b_tr", "b_av", "b_aot", "b_wo",
             "f_ln", "f_xt", "f_up", "f_ht", "f_down", "x_ln", "x_xt", "x_g"]
            + [(k, b, c) for b in range(2) for c in range(DC) for k in ("x_s", "x_tr", "x_av")]
            + ["x_zt", "x_o"])
C_STAGES = ["c_ln", "c_xt", "c_qkv", "c_s", "c_tr", "c_av", "c_aot", "c_wo",
            "m_ln", "m_xt", "m_gu", "m_out"]


STAGE_NAMES = {s[0] if isinstance(s, tuple) else s for s in A_STAGES + B_STAGES + C_STAGES}


def merged(*lists):
    keyed = [((n + 0.5) / len(stages), k, s) for k, stages in enumerate(lists) for n, s in enumerate(stages)]
    return [(k, s) for _, k, s in sorted(keyed, key=lambda x: x[:2])]


def build(nc, a):
    TILES = a["x"].shape[0] // P
    assert TILES % 2 == 0 and TILES >= 6

    ctx = ExitStack()
    with ctx:
        def sb(name, shape, dt=F32):
            return ctx.enter_context(nc.sbuf_tensor(name, shape, dt))

        def sem(name):
            return ctx.enter_context(nc.semaphore(name))

        def scratch(name, shape, dt=F32):
            return nc.dram_tensor(name, shape, dt, kind="Internal").ap()

        expert_in = scratch("expert_in", (E * CAP, D))
        expert_out = scratch("expert_out", (E * CAP, D))
        partial = scratch("partial", (TILES * P, D))
        route_slot = scratch("route_slot", (TILES * P, TOPK), I32)
        route_gate = scratch("route_gate", (TILES * P, TOPK))

        psS = [ctx.enter_context(nc.psum_tensor(f"psS{n}", [P, 512], F32)) for n in range(2)]
        psW = [ctx.enter_context(nc.psum_tensor(f"psW{n}", [P, 512], F32)) for n in range(2)]
        psB = ctx.enter_context(nc.psum_tensor("psB", [P, 2, 512], F32))
        psC = ctx.enter_context(nc.psum_tensor("psC", [P, 2, 512], F32))

        class Area:

            def __init__(self, buffer):
                self.buffer, self.at = buffer, 0

            def cut(self, *shape, dt=F32):
                n = int(np.prod(shape)) * (2 if dt == BF16 else 4) // 4
                piece = self.buffer[:, self.at:self.at + n]
                self.at += n
                if dt != F32:
                    piece = piece.bitcast(dt)
                dims = "abcd"[:len(shape)]
                if len(shape) == 1:
                    return piece
                return piece.rearrange(f"p ({' '.join(dims)}) -> p {' '.join(dims)}",
                                       **{k: v for k, v in zip(dims, shape)})

        qk = sb("qk", [P, DC, 2, H, S])
        zT = sb("zT", [P, DC, H, 2, S])
        qk_flat = qk[:].rearrange("p c b h s -> p (c b h s)")
        raw = zT[:].rearrange("p c h b s -> p (c h b s)")
        setup = Area(qk_flat)

        once = []

        def const(name, shape, src, dt=F32):
            t = sb(name, shape, dt)
            once.append((t[:], src))
            return t

        def const_for_setup(shape, src, dt=F32):
            t = setup.cut(*shape, dt=dt)
            once.append((t, src))
            return t

        def spread(v, n):
            return v.rearrange("(a n) -> a n", a=1).broadcast_to([P, n])

        def chunked(w):
            return w.rearrange("(c p) n -> p c n", p=P)

        ident = const("ident", [P, P], a["c_ident"])
        head_mask = const("head_mask", [P, 4], a["c_head_mask"])
        before = const_for_setup([P], a["c_before"])
        expert_no = const("expert_no", [P, E], a["c_expert_no"])
        rope_cos = const("rope_cos", [P, 2 * D], a["c_rope_cos"])
        rope_sin = const("rope_sin", [P, 2 * D], a["c_rope_sin"])
        alibi = const("alibi", [P, PAIRS * S], a["c_alibi"])
        wq = const("wq", [P, DC, H * DH], chunked(a["L0_xattn_Wq"]))
        wkT = const("wkT", [P, PAIRS, D], chunked(a["L0_xattn_WkT"]))
        wv = const("wv", [P, DC, H * DH], chunked(a["L0_xattn_Wv"]))
        wo = const("wo", [P, PAIRS, D], chunked(a["L0_xattn_Wo"]))
        bqkv = sb("bqkv", [P, 3 * D])
        wqkv_b = sb("wqkv_b", [P, DC, 3 * D])
        for n, k in enumerate("qkv"):
            once.append((wqkv_b[:, :, n * D:(n + 1) * D], chunked(a["L0_attn_w" + k])))
            once.append((bqkv[:, n * D:(n + 1) * D], spread(a["L0_attn_b" + k], D)))
        wo_b = const("wo_b", [P, DC, D], chunked(a["L0_attn_wo"]))
        bo_b = const("bo_b", [P, D], spread(a["L0_attn_bo"], D))
        norm1 = const("norm1", [P, D], spread(a["L0_ffn_norm1_w"], D))
        norm2 = const("norm2", [P, FF], spread(a["L0_ffn_norm2_w"], FF))
        act_sc = const("act_sc", [P, 1], spread(a["L0_ffn_act_scale"], 1))
        act_bi = const("act_bi", [P, 1], spread(a["L0_ffn_act_bias"], 1))
        woT_x = const_for_setup([DC, D], chunked(a["L1_xattn_WoT"]))
        bo_x = const("bo_x", [P, D], spread(a["L1_xattn_bo"], D))
        w_c = sb("w_c", [P, DC, 3 * D])
        for n, k in enumerate("qkv"):
            once.append((w_c[:, :, n * D:(n + 1) * D], chunked(a["L1_attn_W" + k])))
        bqk_c = sb("bqk_c", [P, 2, DC])
        for n, k in enumerate("qk"):
            once.append((bqk_c[:, n, :], a["L1_attn_b" + k]))
        bv_c = const("bv_c", [P, D], spread(a["L1_attn_bv"], D))
        wo_c = const("wo_c", [P, DC, D], chunked(a["L1_attn_Wo"]))
        bo_c = const("bo_c", [P, D], spread(a["L1_attn_bo"], D))
        gate_bias = const("gate_bias", [P, E], spread(a["L1_ffn_bias"], E))
        gate_bf = const_for_setup([DC, E], chunked(a["L1_ffn_gate_wT"]), BF16)
        sw13_bf = setup.cut(DC, 2 * EI, dt=BF16)
        once.append((sw13_bf[:, :, 0:EI], chunked(a["L1_ffn_sw1T"])))
        once.append((sw13_bf[:, :, EI:2 * EI], chunked(a["L1_ffn_sw3T"])))
        sw2_bf = const_for_setup([D], a["L1_ffn_sw2T"], BF16)
        diag = setup.cut(3, P)
        diag_loads = [(diag[HD * h:HD * h + HD, n, HD * h:HD * h + HD], a["L1_xattn_W" + k])
                      for n, k in enumerate("qkv") for h in range(P // HD)]

        identb = sb("identb", [P, P], BF16)
        beforeb = sb("beforeb", [P, P], BF16)
        onesb = sb("onesb", [P, P], BF16)
        ones = sb("ones", [P, P])
        neg_half = sb("neg_half", [P, 1])
        carrier = sb("carrier", [P, 2])
        up_w = sb("up_w", [P, DC, FF], BF16)
        down_w = sb("down_w", [P, FF // P, D], BF16)
        wsum = sb("wsum", [P, 2])
        wmean = sb("wmean", [P, 2])
        wscale = sb("wscale", [P, 2])
        wdeq = sb("wdeq", [P, 2])
        gx = sb("gx", [P, P])
        vo = sb("vo", [P, DC, D])
        gate_w = sb("gate_w", [P, DC, E])
        sw13 = sb("sw13", [P, DC, 2 * EI])
        sw2 = sb("sw2", [P, D])
        
        xa = sb("xa", [P, 2, D])
        cx = sb("cx", [P, 2, 2 * KC, D])
        cxT = sb("cxT", [P, 2, DC, 2, CTX])
        xnA, xnTA = sb("xnA", [P, D]), sb("xnTA", [P, DC, P])
        stA = sb("stA", [P, 16])
        qT = sb("qT", [P, PAIRS, P])
        prA = sb("prA", [P, 2, 2, CTX])
        prTA = sb("prTA", [P, 2, KC, 2 * P])
        smA = sb("smA", [P, 2, 3, 2])
        oT = qT
        up_raw = raw[:, 0:DC * FF].rearrange("p (c n) -> p c n", c=DC)
        down_raw = raw[:, DC * FF:2 * DC * FF].rearrange("p (c n) -> p c n", n=D)
        once.append((up_raw, chunked(a["L0_ffn_w1T"])))
        once.append((down_raw, chunked(a["L0_ffn_w2T"])))
        xb = sb("xb", [P, 2, D])
        mask = sb("mask", [P, 2, 2, CTX], I32)
        mask_add = sb("mask_add", [P, 2, CTX])
        xnB, xnTB = sb("xnB", [P, D]), sb("xnTB", [P, DC, P])
        stB = sb("stB", [P, 32])
        qkB = sb("qkB", [P, 2 * D])
        vB = sb("vB", [P, D])
        kTB = sb("kTB", [P, DC, P])
        prB = sb("prB", [P, 2, 4, 2 * S])
        smB = sb("smB", [P, 3, 16])
        aoB, aoTB = sb("aoB", [P, D]), sb("aoTB", [P, DC, P])
        hid = sb("hid", [P, FF])
        hq = sb("hq", [P, FF], BF16)
        sq = sb("sq", [P, FF])
        qcos, rot = hid[:, 0:2 * D], sq[:, 0:2 * D]
        qBB = sq[:].rearrange("p (c b m s) -> p c b m s", c=DC, b=2, m=4)
        prTB = hid[:].rearrange("p (g c n) -> p g c n", g=2, c=4)
        g2 = prB[:].rearrange("p g c n -> p (g c n)")
        hqT = sb("hqT", [P, FF // P, P], BF16)
        xc = sb("xc", [P, 2, D])
        xnC, xnTC = sb("xnC", [P, D]), sb("xnTC", [P, DC, P])
        xnM = sb("xnM", [P, 2, D])
        stC = sb("stC", [P, 16])
        vC = sb("vC", [P, D])
        kTC = sb("kTC", [P, DC, P])
        qBC = sb("qBC", [P, DC, 2, 4, S])
        prC = sb("prC", [P, 2, 4, 2 * S])
        smC = sb("smC", [P, 3, 16])
        prTC = sb("prTC", [P, 2, 4, P])
        aoC, aoTC = sb("aoC", [P, D]), sb("aoTC", [P, DC, P])
        shared = sb("shared", [P, 2, P])
        gl = sb("gl", [P, 3, E])
        top = sb("top", [P, 8])
        topi = sb("topi", [P, 8], U32)
        topf = sb("topf", [P, 8])
        hot = sb("hot", [P, TOPK, E])
        hot2 = sb("hot2", [P, TOPK, E])
        sel = sb("sel", [P, E], BF16)
        seen = sb("seen", [P, E], BF16)
        rt = sb("rt", [P, 10, TOPK])
        gate = sb("gate", [P, 2, TOPK])
        slot = sb("slot", [P, 2, TOPK], I32)
        put = sb("put", [P, 2, TOPK], I32)
        part = sb("part", [P, 2, D])

        s_once, s_diag, s_zero = sem("s_once"), sem("s_diag"), sem("s_zero")
        s_setup_dve, s_setup_act = sem("s_setup_dve"), sem("s_setup_act")
        s_setup_pe, s_setup_pool = sem("s_setup_pe"), sem("s_setup_pool")
        in_x = [sem(f"in_x{n}") for n in range(2)]
        in_cx = [sem(f"in_cx{n}") for n in range(2)]
        in_mask = [sem(f"in_mask{n}") for n in range(2)]
        out_part = [sem(f"out_part{n}") for n in range(2)]
        scattered = [sem(f"scattered{n}") for n in range(2)]
        late = Area(qk_flat)
        ex_x, ex_y = late.cut(2, KC, D), late.cut(2, KC, D)
        fin_rows = late.cut(2, TOPK, D)
        late = Area(raw)
        ex_w13, ex_w2 = late.cut(2, DC, 2 * EI, dt=BF16), late.cut(2, D, dt=BF16)
        ex_w13f, ex_w2f = late.cut(DC, 2 * EI), late.cut(D)
        ex_xT, ex_h = late.cut(DC, CAP), late.cut(2, CAP)
        fin, fin_slot, fin_gate = late.cut(2, D), late.cut(2, TOPK, dt=I32), late.cut(2, TOPK)

        front = Chain(sem("front"), NORM + QKV_A)
        tail = Chain(sem("tail"), ["v_ps", ("oT", 2), "y_ps", "x1"])
        scores_ps = Signal(sem("scores_ps"), UNITS)
        neg_max = Signal(sem("neg_max"), UNITS)
        exp_done = Signal(sem("exp_done"), UNITS)
        inv_sum = Signal(sem("inv_sum"), UNITS)
        probs = Signal(sem("probs"), UNITS)
        probsT_ps = Signal(sem("probsT_ps"), UNITS)
        probsT = Signal(sem("probsT"), UNITS)
        mixed_ps = Signal(sem("mixed_ps"), UNITS)
        mixed = Signal(sem("mixed"), UNITS)
        rope = Chain(sem("rope"), ROPE_ATTN)
        rope_sums = Chain(sem("rope_sums"), [("sum", 2), "inverse"])
        alib_sums = Chain(sem("alib_sums"), [("sum", 2), "inverse"])
        masked_sums = Signal(sem("masked_sums"), 4)
        ffn = Chain(sem("ffn"), FFN)
        masked = Chain(sem("masked"), MASKED)
        mask_ready = Signal(sem("mask_ready"), 1)
        alib = Chain(sem("alib"), ALIBI_ATTN)
        route = Chain(sem("route"), ROUTE)
        ex_in = [sem(f"ex_in{n}") for n in range(2)]
        ex = Chain(sem("ex"), ["weights", "xT_ps", ("xT", 2), "up_ps", "exp", "plus1", "inverse", "silu", "h",
                               "down_ps", ("y", 2)])
        ex_out = [sem(f"ex_out{n}") for n in range(2)]
        sum_in = [sem(f"sum_in{n}") for n in range(2)]
        sum_rows = [sem(f"sum_rows{n}") for n in range(2)]
        summed = Chain(sem("summed"), [("sum", TOPK)])
        sum_out = [sem(f"sum_out{n}") for n in range(2)]

        block = ctx.enter_context(nc.Block())
        ORDER = merged(A_STAGES, B_STAGES, C_STAGES)

        def run(eng, stages, extra=None):
            def body(t):
                for stream, stage in ORDER:
                    name, args = (stage[0], stage[1:]) if isinstance(stage, tuple) else (stage, ())
                    tile = t.back(stream)
                    if name in stages and tile.exists and (tile.i is not None or tile.c < TILES):
                        stages[name](tile, *args)
                if extra is not None:
                    extra(t)
            for c in range(3):
                body(Tile(c))
            with eng.Fori(0, (TILES - 4) // 2) as i:
                body(Tile(3, i))
                body(Tile(4, i))
            for c in range(TILES - 1, TILES + 2):
                body(Tile(c))

        @block.sync
        def _(sp):
            for dst, src in once:
                sp.dma_start(dst, src).then_inc(s_once, 16)
            sp.wait_ge(s_setup_pool, 2)
            for dst, src in diag_loads:
                sp.dma_start(dst, src).then_inc(s_diag, 16)

            def load(t):
                p = t.par
                rows = bass.ts(t.row(), P)
                samples = bass.ts(t.row(), 2)
                after(sp, tail, t.back(2), "x1")
                sp.dma_start(xa[:, p, :], a["x"][rows, :]).then_inc(in_x[p], 16)
                after(sp, masked, t.back(2), "biased")
                sp.dma_start(cx[:, p], a["ctx"][samples].rearrange("b (k p) d -> p (b k) d", p=P)).then_inc(in_cx[p], 16)
                for b in range(2):
                    sp.dma_start(cxT[:, p, :, b, :], a["ctxT"][t.row() * 2 + b].rearrange("(c p) k -> p c k", p=P)
                                 ).then_inc(in_cx[p], 16)
                for half in range(2):
                    sp.dma_start(mask[S * half:S * half + S, p], a["mask"][samples].rearrange("b q k -> q b k")
                                 ).then_inc(in_mask[p], 16)

            def store(t):
                p = t.par
                rows = bass.ts(t.row(), P)
                after(sp, route, t, "put")
                sp.dma_start(partial[rows, :], part[:, p, :]).then_inc(out_part[p], 16)
                sp.dma_start(route_slot[rows, :], slot[:, p, :]).then_inc(out_part[p], 16)
                sp.dma_start(route_gate[rows, :], gate[:, p, :]).then_inc(out_part[p], 16)

            def traffic(t):
                if t.i is not None or t.c + 1 < TILES:
                    load(t.back(-1))
                if t.back(2).exists:
                    store(t.back(2))

            load(Tile(0))
            run(sp, {}, traffic)

            for p in range(2):
                sp.wait_ge(scattered[p], 16 * TOPK * (TILES // 2))

            def load_expert(e):
                p = e.par
                after(sp, ex, e.back(2), "y")
                r = e.row()
                sp.dma_start(ex_x[:, p], expert_in[bass.ts(r, CAP), :].rearrange("(k p) d -> p k d", p=P)
                             ).then_inc(ex_in[p], 16)
                sp.dma_start(ex_w13[:, p, :, 0:EI], a["L1_ffn_W1"][bass.ts(r, D), :].rearrange("(c p) n -> p c n", p=P)
                             ).then_inc(ex_in[p], 16)
                sp.dma_start(ex_w13[:, p, :, EI:], a["L1_ffn_W3"][bass.ts(r, D), :].rearrange("(c p) n -> p c n", p=P)
                             ).then_inc(ex_in[p], 16)
                sp.dma_start(ex_w2[:, p], a["L1_ffn_W2"][bass.ts(r, EI), :]).then_inc(ex_in[p], 16)

            def store_expert(e):
                p = e.par
                after(sp, ex, e, "y")
                sp.dma_start(expert_out[bass.ts(e.row(), CAP), :].rearrange("(k p) d -> p k d", p=P), ex_y[:, p]
                             ).then_inc(ex_out[p], 16)

            load_expert(Tile(0))
            load_expert(Tile(1))
            store_expert(Tile(0))
            with sp.Fori(0, (E - 2) // 2) as i:
                for c in (2, 3):
                    load_expert(Tile(c, i))
                    store_expert(Tile(c - 1, i))
            store_expert(Tile(E - 1))

            for p in range(2):
                sp.wait_ge(out_part[p], 16 * 3 * (TILES // 2))

            def load_sum(t):
                p = t.par
                rows = bass.ts(t.row(), P)
                after(sp, summed, t.back(2), "sum")
                if t.back(2).exists:
                    sp.wait_ge(sum_out[p], t.back(2).loads())
                sp.dma_start(fin[:, p, :], partial[rows, :]).then_inc(sum_in[p], 16)
                sp.dma_start(fin_slot[:, p, :], route_slot[rows, :]).then_inc(sum_in[p], 16)
                sp.dma_start(fin_gate[:, p, :], route_gate[rows, :]).then_inc(sum_in[p], 16)

            def store_sum(t):
                after(sp, summed, t, "sum")
                sp.dma_start(a["out"][bass.ts(t.row(), P), :], fin[:, t.par, :]).then_inc(sum_out[t.par], 16)

            load_sum(Tile(0))
            load_sum(Tile(1))
            store_sum(Tile(0))
            with sp.Fori(0, (TILES - 2) // 2) as i:
                for c in (2, 3):
                    load_sum(Tile(c, i))
                    store_sum(Tile(c - 1, i))
            store_sum(Tile(TILES - 1))
            for p in range(2):
                sp.wait_ge(sum_out[p], 16 * (TILES // 2))

        @block.tensor
        def _(pe):
            def mm(out, lhsT, rhs, first, last, **kw):
                return pe.matmul(out, lhsT, rhs, start=first, stop=last, **kw)

            pe.wait_ge(s_once, 16 * len(once))
            pe.wait_ge(s_diag, 16 * len(diag_loads))
            pe.wait_ge(s_setup_pool, 7)
            pe.wait_ge(s_setup_dve, 2)
            mm(psW[0][:, 0:2], ones[:], wsum[:], True, True)
            mm(psW[0][:, P:2 * P], diag[:, 0, :], diag[:, 1, :], True, True).then_inc(s_setup_pe, 1)
            for c in range(DC):
                ins = mm(psW[1][:, c * D:(c + 1) * D], diag[:, 2, :], woT_x[:, c, :], True, True)
            ins.then_inc(s_setup_pe, 1)
            pe.wait_ge(s_setup_dve, 14)
            pe.wait_ge(s_setup_act, 3)

            def turn(out, src, n=DC):
                for c in range(n):
                    ins = pe.transpose(out[:, c * P:(c + 1) * P], src[:, c * P:(c + 1) * P], ident[:])
                return ins

            def project(out, lhsT, rhs):
                for c in range(DC):
                    ins = mm(out, lhsT[:, c, :], rhs[:, c, :], c == 0, c == DC - 1)
                return ins

            def a_xt(t):
                after(pe, front, t, "xn")
                turn(psW[0][:, 0:D], xnA[:]).then_inc(front.sem, 1)

            def a_q(t):
                after(pe, front, t, "xnT")
                for j in range(PAIRS):
                    ins = project(psW[j // 4][:, (j % 4) * P:(j % 4 + 1) * P], wq[:, :, j * P:(j + 1) * P], xnTA)
                ins.then_inc(front.sem, 1)

            def a_qp(t, c, g):
                n = 2 * c + g
                after(pe, front, t, f"qk{n - 1}" if n else "qT")
                for j in range(4):
                    for half in range(2):
                        rows = slice(DH * half, DH * half + DH)
                        ins = mm(psW[half][:, j * P:(j + 1) * P], wkT[rows, 4 * g + j, c * P:(c + 1) * P],
                                 qT[rows, 4 * g + j, :], True, True)
                ins.then_inc(front.sem, 1)

            def a_s(t, u):
                b, quarter = divmod(u, 4)
                if u == 0:
                    after(pe, front, t, "qk3")
                    pe.wait_ge(in_cx[t.par], t.landed(3))
                if u >= 2:
                    after(pe, exp_done, t, u - 2)
                for k in range(2):
                    j = 2 * quarter + k
                    for c in range(DC):
                        ins = mm(psS[u % 2][:, k * CTX:(k + 1) * CTX], qk[:, c, b, 2 * j:2 * j + 2, :],
                                 cxT[:, t.par, c, b, :], c == 0, c == DC - 1)
                ins.then_inc(scores_ps.sem, 1)

            def a_tr(t, u):
                after(pe, probs, t, u)
                for kc in range(KC):
                    for k in range(2):
                        ins = pe.transpose(psW[0][:, (2 * kc + k) * P:(2 * kc + k + 1) * P],
                                           prA[:, u % 2, k, kc * P:(kc + 1) * P], ident[:])
                ins.then_inc(probsT_ps.sem, 1)

            def a_z(t, u):
                b = u // 4
                after(pe, probsT, t, u)
                if u:
                    after(pe, mixed, t, u - 1)
                for c in range(DC):
                    for kc in range(KC):
                        ins = mm(psW[1][:, c * 2 * P:(c + 1) * 2 * P], cx[:, t.par, b * KC + kc, c * P:(c + 1) * P],
                                 prTA[:, u % 2, kc, :], kc == 0, kc == KC - 1)
                ins.then_inc(mixed_ps.sem, 1)

            def a_v(t):
                after(pe, mixed, t, UNITS - 1)
                for h in range(H):
                    rows = slice(DH * (h % 2), DH * (h % 2) + DH)
                    j = h // 2
                    for c in range(DC):
                        ins = mm(psW[j // 4][rows, (j % 4) * P:(j % 4 + 1) * P], wv[:, c, h * DH:(h + 1) * DH],
                                 zT[:, c, h, :, :], c == 0, c == DC - 1)
                ins.then_inc(tail.sem, 1)

            def a_y(t):
                after(pe, tail, t, "oT")
                for j in range(PAIRS):
                    ins = mm(psW[0][:, 0:D], oT[:, j, :], wo[:, j, :], j == 0, j == PAIRS - 1)
                ins.then_inc(tail.sem, 1)

            def scores_small(ps, q, k):
                for c in range(DC):
                    for s in range(2):
                        for b in range(2):
                            for g in range(2):
                                rows = slice(S * g, S * g + S)
                                at = ((c * 2 + s) * 2 + b) * S
                                ins = mm(ps[:, g, at:at + S], q[rows, c, b, 2 * s:2 * s + 2, :],
                                         k[rows, c, b * S:(b + 1) * S], True, True)
                return ins

            def probs_turn(ps, pr):
                for g in range(2):
                    for cs in range(4):
                        ins = pe.transpose(ps[:, g, cs * P:(cs + 1) * P], pr[:, g, cs, :], ident[:])
                return ins

            def values_small(ps, prT, v):
                for c in range(DC):
                    for g in range(2):
                        for s in range(2):
                            j = 4 * c + 2 * g + s
                            for b in range(2):
                                rows = slice(S * b, S * b + S)
                                ins = mm(ps[:, b, j * 2 * HD:(j + 1) * 2 * HD], prT[rows, g, 2 * c + s, :],
                                         v[rows, j * 2 * HD:(j + 1) * 2 * HD], True, True)
                return ins

            def b_xt(t):
                after(pe, rope, t, "xn")
                after(pe, masked, t.back(1), "biased")
                turn(psB[:, 0, 0:D], xnB[:]).then_inc(rope.sem, 1)

            def b_qkv(t):
                after(pe, rope, t, "xnT")
                project(psB[:, 0, :], xnTB, wqkv_b[:, :, 0:2 * D])
                project(psB[:, 1, 0:D], xnTB, wqkv_b[:, :, 2 * D:3 * D]).then_inc(rope.sem, 1)

            def b_qkt(t):
                after(pe, rope, t, "roped")
                turn(psB[:, 0, 0:D], qkB[:, 0:D])
                turn(psB[:, 1, 0:D], qkB[:, D:2 * D]).then_inc(rope.sem, 1)

            def b_s(t):
                after(pe, rope, t, "qkT")
                scores_small(psB, qBB, kTB).then_inc(rope.sem, 1)

            def b_tr(t):
                after(pe, rope, t, "exp")
                probs_turn(psB, prB).then_inc(rope.sem, 1)

            def b_av(t):
                after(pe, rope, t, "pT")
                values_small(psB, prTB, vB).then_inc(rope.sem, 1)

            def b_aot(t):
                after(pe, rope, t, "heads")
                turn(psB[:, 0, 0:D], aoB[:]).then_inc(rope.sem, 1)

            def b_wo(t):
                after(pe, rope, t, "headsT")
                project(psB[:, 1, 0:D], aoTB, wo_b).then_inc(rope.sem, 1)

            def f_xt(t):
                after(pe, ffn, t, "in_quant")
                out = psB[:, 0, :].bitcast(BF16)
                for c in range(DC):
                    ins = pe.transpose(out[:, c * P:(c + 1) * P], hq[:, c * P:(c + 1) * P], identb[:])
                ins.then_inc(ffn.sem, 1)

            def f_up(t):
                after(pe, ffn, t, "inT")
                for n in range(2):
                    for c in range(DC):
                        ins = mm(psB[:, n, :], hqT[:, c, :], up_w[:, c, n * 512:(n + 1) * 512], c == 0, c == DC - 1)
                ins.then_inc(ffn.sem, 1)

            def f_ht(t):
                after(pe, ffn, t, "mid_quant")
                out = psB[:, 0, :].bitcast(BF16)
                for c in range(FF // P):
                    ins = pe.transpose(out[:, c * P:(c + 1) * P], hq[:, c * P:(c + 1) * P], identb[:])
                ins.then_inc(ffn.sem, 1)

            def f_down(t):
                after(pe, ffn, t, "midT")
                for c in range(FF // P):
                    ins = mm(psB[:, 1, 0:D], hqT[:, c, :], down_w[:, c, :], c == 0, c == FF // P - 1)
                ins.then_inc(ffn.sem, 1)

            def x_xt(t):
                after(pe, masked, t, "xn")
                turn(psB[:, 0, 0:D], xnB[:]).then_inc(masked.sem, 1)

            def x_g(t):
                after(pe, masked, t, "xnT")
                for c in range(DC):
                    ins = mm(psB[:, 0, c * P:(c + 1) * P], gx[:], xnTB[:, c, :], True, True)
                ins.then_inc(masked.sem, 1)

            def x_s(t, b, c):
                u = 2 * b + c
                after(pe, masked, t, f"heads{u - 1}" if u else "q")
                for s in range(2):
                    for g in range(2):
                        rows = slice(S * g, S * g + S)
                        ins = mm(psB[:, g, s * CTX:(s + 1) * CTX], qBB[rows, c, b, 2 * s:2 * s + 2, :],
                                 cxT[rows, t.par, c, b, :], True, True)
                ins.then_inc(masked.sem, 1)

            def x_tr(t, b, c):
                u = 2 * b + c
                after(pe, masked, t, f"exp{u}")
                for g in range(2):
                    for sk in range(4):
                        ins = pe.transpose(psB[:, g, sk * P:(sk + 1) * P], prB[:, g, sk, :], ident[:])
                ins.then_inc(masked.sem, 1)

            def x_av(t, b, c):
                u = 2 * b + c
                after(pe, masked, t, f"pT{u}")
                for g in range(2):
                    for s in range(2):
                        j = 4 * c + 2 * g + s
                        for kc in range(KC):
                            ins = mm(psB[:, 0, (2 * g + s) * 2 * HD:(2 * g + s + 1) * 2 * HD], prTB[:, g, 2 * s + kc, :],
                                     cx[:, t.par, b * KC + kc, j * 2 * HD:(j + 1) * 2 * HD], kc == 0, kc == KC - 1)
                ins.then_inc(masked.sem, 1)

            def x_zt(t):
                after(pe, masked, t, "heads3")
                turn(psB[:, 0, 0:D], aoB[:]).then_inc(masked.sem, 1)

            def x_o(t):
                after(pe, masked, t, "headsT")
                project(psB[:, 1, 0:D], aoTB, vo).then_inc(masked.sem, 1)

            def c_xt(t):
                after(pe, alib, t, "xn")
                after(pe, route, t.back(1), "put")
                turn(psC[:, 0, 0:D], xnC[:]).then_inc(alib.sem, 1)

            def c_qkv(t):
                after(pe, alib, t, "xnT")
                for c in range(DC):
                    project(psC[:, 0, c * P:(c + 1) * P], w_c[:, :, c * P:(c + 1) * P], xnTC)
                project(psC[:, 0, D:2 * D], xnTC, w_c[:, :, 2 * D:3 * D])
                for c in range(DC):
                    ins = project(psC[:, 1, c * P:(c + 1) * P], w_c[:, :, D + c * P:D + (c + 1) * P], xnTC)
                ins.then_inc(alib.sem, 1)

            def c_s(t):
                after(pe, alib, t, "qkv")
                scores_small(psC, qBC, kTC).then_inc(alib.sem, 1)

            def c_tr(t):
                after(pe, alib, t, "exp")
                probs_turn(psC, prC).then_inc(alib.sem, 1)

            def c_av(t):
                after(pe, alib, t, "pT")
                values_small(psC, prTC, vC).then_inc(alib.sem, 1)

            def c_aot(t):
                after(pe, alib, t, "heads")
                turn(psC[:, 0, 0:D], aoC[:]).then_inc(alib.sem, 1)

            def c_wo(t):
                after(pe, alib, t, "headsT")
                project(psC[:, 1, 0:D], aoTC, wo_c).then_inc(alib.sem, 1)

            def m_xt(t):
                after(pe, route, t, "xn")
                turn(psC[:, 0, 0:D], xnM[:, t.par, :]).then_inc(route.sem, 1)

            def m_gu(t):
                after(pe, route, t, "xnT")
                for n in range(2):
                    project(psC[:, 0, n * P:(n + 1) * P], sw13[:, :, n * P:(n + 1) * P], xnTC)
                project(psC[:, 1, 0:E], xnTC, gate_w).then_inc(route.sem, 1)

            def m_out(t):
                after(pe, route, t, "gates")
                mm(psC[:, 1, 0:E], beforeb[:], sel[:], True, False)
                mm(psC[:, 1, 0:E], onesb[:], seen[:], False, True)
                mm(psC[:, 0, 0:D], shared[:, 1, :], sw2[:], True, True).then_inc(route.sem, 1)

            run(pe, {k: v for k, v in locals().items() if k in STAGE_NAMES})

            def expert(e):
                p = e.par
                pe.wait_ge(ex_in[p], e.landed(4))
                after(pe, ex, e.back(1), "y")
                for k in range(KC):
                    for c in range(DC):
                        ins = pe.transpose(psB[:, 0, (2 * c + k) * P:(2 * c + k + 1) * P],
                                           ex_x[:, p, k, c * P:(c + 1) * P], ident[:])
                ins.then_inc(ex.sem, 1)
                after(pe, ex, e, "xT")
                for n in range(2):
                    for c in range(DC):
                        ins = mm(psB[:, 1, n * CAP:(n + 1) * CAP], ex_w13f[:, c, n * EI:(n + 1) * EI],
                                 ex_xT[:, c, :], c == 0, c == DC - 1)
                ins.then_inc(ex.sem, 1)
                after(pe, ex, e, "h")
                for k in range(KC):
                    ins = mm(psC[:, 0, k * D:(k + 1) * D], ex_h[:, 1, k * P:(k + 1) * P], ex_w2f, True, True)
                ins.then_inc(ex.sem, 1)

            expert(Tile(0))
            expert(Tile(1))
            with pe.Fori(0, (E - 2) // 2) as i:
                expert(Tile(2, i))
                expert(Tile(3, i))

        @block.scalar
        def _(act):
            copy = lambda out, in_: act.activation(out, in_, ACT.Copy)
            act.wait_ge(s_once, 16 * len(once))
            copy(gate_w[:], gate_bf).then_inc(s_setup_act, 1)
            copy(sw13[:], sw13_bf).then_inc(s_setup_act, 1)
            copy(sw2[:], sw2_bf).then_inc(s_setup_act, 1)
            act.wait_ge(s_setup_pool, 4)
            zero_rows = expert_in.rearrange("(n p r) d -> n p (r d)", p=P, r=4)
            for n in range(E * CAP // (4 * P)):
                act.dma_start(zero_rows[n], hid[:]).then_inc(s_zero, 16)

            def a_xt(t):
                after(act, front, t, "xnT_ps")
                copy(xnTA[:].rearrange("p c n -> p (c n)"), psW[0][:, 0:D]).then_inc(front.sem, 1)

            def a_q(t):
                after(act, front, t, "qT_ps")
                act.activation(qT[:, 0:4, :].rearrange("p j n -> p (j n)"), psW[0][:], ACT.Copy,
                               scale=DH ** -0.5).then_inc(front.sem, 1)

            def a_qp(t, c, g):
                after(act, front, t, f"qk_ps{2 * c + g}")
                copy(qk[:, c, :, 8 * g:8 * g + 8:2, :].rearrange("p b h s -> p h b s"),
                     psW[0][:].rearrange("p (h b s) -> p h b s", h=4, b=2)).then_inc(front.sem, 1)

            def a_s(t, u):
                after(act, neg_max, t, u)
                for k in range(2):
                    ins = act.activation(prA[:, u % 2, k, :], psS[u % 2][:, k * CTX:(k + 1) * CTX], ACT.Exp,
                                         bias=smA[:, u % 2, 0, k:k + 1], accum_out=smA[:, u % 2, 1, k:k + 1])
                ins.then_inc(exp_done.sem, 1)

            def a_tr(t, u):
                after(act, probsT_ps, t, u)
                if u >= 2:
                    after(act, mixed_ps, t, u - 2)
                copy(prTA[:, u % 2].rearrange("p k n -> p (k n)"), psW[0][:]).then_inc(probsT.sem, 1)

            def a_v(t):
                after(act, tail, t, "v_ps")
                copy(oT[:, 0:4, :].rearrange("p j n -> p (j n)"), psW[0][:]).then_inc(tail.sem, 1)

            def flat(x):
                return x[:].rearrange("p c n -> p (c n)")

            def b_xt(t):
                after(act, rope, t, "xnT_ps")
                copy(flat(xnTB), psB[:, 0, 0:D]).then_inc(rope.sem, 1)

            def b_qkt(t):
                after(act, rope, t, "qkT_ps")
                copy(flat(kTB), psB[:, 1, 0:D]).then_inc(rope.sem, 1)

            def b_s(t):
                after(act, rope, t, "shifted")
                act.activation(prB[:], prB[:], ACT.Exp, scale=HD ** -0.5).then_inc(rope.sem, 1)

            def b_tr(t):
                after(act, rope, t, "pT_ps")
                copy(prTB[:, 0].rearrange("p c n -> p (c n)"), psB[:, 0, :]).then_inc(rope.sem, 1)

            def b_aot(t):
                after(act, rope, t, "headsT_ps")
                copy(flat(aoTB), psB[:, 0, 0:D]).then_inc(rope.sem, 1)

            def squares(t, src, before_, dst):
                after(act, ffn, t, before_)
                act.activation(sq[:, 0:src.shape[-1]], src, ACT.Square, accum_out=dst).then_inc(ffn.sem, 1)

            def f_ln(t):
                squares(t, xnB[:], "xn", stB[:, 16:17])

            def f_xt(t):
                after(act, ffn, t, "inT_ps")
                copy(hqT[:, 0:DC, :].rearrange("p c n -> p (c n)"), psB[:, 0, :].bitcast(BF16)[:, 0:D]).then_inc(ffn.sem, 1)

            def f_up(t):
                after(act, ffn, t, "up_ps")
                for n in range(2):
                    act.activation(hid[:, n * 512:(n + 1) * 512], psB[:, n, :], ACT.Relu,
                                   scale=stB[:, 22:23]).then_inc(ffn.sem, 1)
                after(act, ffn, t, "relu")
                act.activation(hid[:], hid[:], ACT.Square).then_inc(ffn.sem, 1)
                squares(t, hid[:], "affine", stB[:, 16:17])

            def f_ht(t):
                after(act, ffn, t, "midT_ps")
                copy(hqT[:].rearrange("p c n -> p (c n)"), psB[:, 0, :].bitcast(BF16)).then_inc(ffn.sem, 1)

            def x_xt(t):
                after(act, masked, t, "xnT_ps")
                copy(flat(xnTB), psB[:, 0, 0:D]).then_inc(masked.sem, 1)

            def x_s(t, b, c):
                u = 2 * b + c
                after(act, masked, t, f"offset{u}")
                for g in range(2):
                    for s in range(2):
                        pr = prB[:, g, 2 * s:2 * s + 2, :]
                        n = 2 * g + s
                        act.activation(pr, pr, ACT.Exp, scale=D ** -0.5, bias=smB[:, 1, n:n + 1],
                                       accum_out=smB[:, 2, n:n + 1]).then_inc(masked.sem, 1)

            def x_tr(t, b, c):
                after(act, masked, t, f"pT_ps{2 * b + c}")
                copy(prTB[:, 0].rearrange("p c n -> p (c n)"), psB[:, 0, :]).then_inc(masked.sem, 1)

            def x_zt(t):
                after(act, masked, t, "headsT_ps")
                copy(flat(aoTB), psB[:, 0, 0:D]).then_inc(masked.sem, 1)

            def c_xt(t):
                after(act, alib, t, "xnT_ps")
                copy(flat(xnTC), psC[:, 0, 0:D]).then_inc(alib.sem, 1)

            def c_qkv(t):
                after(act, alib, t, "qkv_ps")
                for c in range(DC):
                    act.activation(kTC[:, c, :], psC[:, 1, c * P:(c + 1) * P], ACT.Identity,
                                   bias=bqk_c[:, 1, c:c + 1]).then_inc(alib.sem, 1)

            def c_s(t):
                after(act, alib, t, "shifted")
                act.activation(prC[:], prC[:], ACT.Exp).then_inc(alib.sem, 1)

            def c_tr(t):
                after(act, alib, t, "pT_ps")
                copy(prTC[:, 0].rearrange("p c n -> p (c n)"), psC[:, 0, :]).then_inc(alib.sem, 1)

            def c_aot(t):
                after(act, alib, t, "headsT_ps")
                copy(flat(aoTC), psC[:, 0, 0:D]).then_inc(alib.sem, 1)

            def m_xt(t):
                after(act, route, t, "xnT_ps")
                copy(flat(xnTC), psC[:, 0, 0:D]).then_inc(route.sem, 1)

            def m_gu(t):
                after(act, route, t, "up_ps")
                act.activation(shared[:, 0, :], psC[:, 0, 0:P], ACT.Exp, scale=-1.0).then_inc(route.sem, 1)
                act.activation(gl[:, 0, :], psC[:, 1, 0:E], ACT.Exp, scale=-1.0).then_inc(route.sem, 1)

            run(act, {k: v for k, v in locals().items() if k in STAGE_NAMES})

            def expert(e):
                p = e.par
                act.wait_ge(ex_in[p], e.landed(4))
                after(act, ex, e.back(1), "y")
                copy(ex_w2f, ex_w2[:, p, :])
                copy(ex_w13f, ex_w13[:, p]).then_inc(ex.sem, 1)
                after(act, ex, e, "xT_ps")
                copy(ex_xT[:, 0, :], psB[:, 0, 0:CAP]).then_inc(ex.sem, 1)
                copy(ex_xT[:, 1, :], psB[:, 0, CAP:2 * CAP]).then_inc(ex.sem, 1)
                after(act, ex, e, "up_ps")
                act.activation(ex_h[:, 0, :], psB[:, 1, 0:CAP], ACT.Exp, scale=-1.0).then_inc(ex.sem, 1)
                after(act, ex, e, "down_ps")
                if e.back(2).exists:
                    act.wait_ge(ex_out[p], e.back(2).loads())
                for k in range(KC):
                    copy(ex_y[:, p, k, :], psC[:, 0, k * D:(k + 1) * D]).then_inc(ex.sem, 1)

            expert(Tile(0))
            expert(Tile(1))
            with act.Fori(0, (E - 2) // 2) as i:
                expert(Tile(2, i))
                expert(Tile(3, i))

        @block.gpsimd
        def _(pool):
            below_last, bound = pool.to_reg(E * CAP - 2), pool.alloc_register("bound")
            pool.memset(diag, 0.0).then_inc(s_setup_pool, 1)
            pool.memset(seen[:], 0.0).then_inc(s_setup_pool, 1)
            pool.memset(neg_half[:], -0.5).then_inc(s_setup_pool, 1)
            pool.memset(hid[:], 0.0).then_inc(s_setup_pool, 1)
            pool.memset(ones[:], 1.0).then_inc(s_setup_pool, 1)
            pool.memset(onesb[:], 1.0).then_inc(s_setup_pool, 1)
            pool.memset(stC[:], 0.0).then_inc(s_setup_pool, 1)

            def rstd(chain, st, name="rstd", src="var", at=8):
                def stage(t):
                    after(pool, chain, t, src)
                    pool.tensor_tensor(st[:, at + 1:at + 2], st[:, at:at + 1], neg_half[:], ALU.pow).then_inc(chain.sem, 1)
                return stage

            a_ln, b_ln, x_ln = rstd(front, stA), rstd(rope, stB), rstd(masked, stB)
            c_ln, m_ln = rstd(alib, stC), rstd(route, stC)

            def f_ln(t):
                rstd(ffn, stB)(t)
                rstd(ffn, stB, src="in_var", at=17)(t)

            def f_up(t):
                rstd(ffn, stB, src="mid_var", at=17)(t)

            def b_qkv(t):
                after(pool, rope, t, "qkv")
                q = qkB[:].rearrange("p (h two e) -> p h two e", two=2, e=HD // 2)
                r = rot.rearrange("p (h two e) -> p h two e", two=2, e=HD // 2)
                sin = rope_sin[:].rearrange("p (h two e) -> p h two e", two=2, e=HD // 2)
                for n in range(2):
                    pool.tensor_tensor(r[:, :, n, :], q[:, :, 1 - n, :], sin[:, :, n, :], ALU.mult).then_inc(rope.sem, 1)

            def x_xt(t):
                pool.wait_ge(in_mask[t.par], t.landed(2))
                after(pool, masked, t.back(1), "biased")
                pool.tensor_tensor(carrier[:, 0:1], neg_half[:], neg_half[:], ALU.add)
                pool.tensor_scalar(mask_add[:], mask[:, t.par], 0.0, -1e20, ALU.is_equal, ALU.mult
                                   ).then_inc(mask_ready.sem, 1)

            def m_out(t):
                if t.i is None and t.c == 0:
                    pool.wait_ge(s_zero, 16 * (E * CAP // (4 * P)))
                after(pool, route, t, "put")
                pool.reg_add(bound, below_last, 1)
                for k in range(TOPK):
                    pool.indirect_dma_start(
                        out=expert_in, out_offset=bass.IndirectOffsetOnAxis(ap=put[:, t.par, k:k + 1].bitcast(U32), axis=0),
                        in_=xnM[:, t.par, :], in_offset=None, bounds_check=bound, oob_is_err=False,
                    ).then_inc(scattered[t.par], 16)

            run(pool, {k: v for k, v in locals().items() if k in STAGE_NAMES})

            for p in range(2):
                pool.wait_ge(ex_out[p], 16 * (E // 2))

            def fetch(t):
                p = t.par
                pool.wait_ge(sum_in[p], t.landed(3))
                after(pool, summed, t.back(2), "sum")
                pool.reg_add(bound, below_last, 1)
                for k in range(TOPK):
                    pool.indirect_dma_start(
                        out=fin_rows[:, p, k, :], out_offset=None, in_=expert_out,
                        in_offset=bass.IndirectOffsetOnAxis(ap=fin_slot[:, p, k:k + 1].bitcast(U32), axis=0),
                        bounds_check=bound, oob_is_err=False).then_inc(sum_rows[p], 16)

            fetch(Tile(0))
            fetch(Tile(1))
            with pool.Fori(0, (TILES - 2) // 2) as i:
                fetch(Tile(2, i))
                fetch(Tile(3, i))

        @block.vector
        def _(dve):
            def carry():
                dve.memset(carrier[:, 1:2], 0.0)

            def wide(x, n):
                return x.unsqueeze(2).broadcast_to([P, x.shape[1], n])

            dve.wait_ge(s_once, 16 * len(once))
            dve.tensor_reduce(wsum[:, 0:1], raw[:, 0:DC * FF], AX.X, ALU.add, apply_absolute_value=True).then_inc(s_setup_dve, 1)
            dve.tensor_reduce(wsum[:, 1:2], raw[:, DC * FF:2 * DC * FF], AX.X, ALU.add, apply_absolute_value=True).then_inc(s_setup_dve, 1)
            dve.wait_ge(s_setup_pe, 2)
            dve.tensor_scalar(wmean[:], psW[0][:, 0:2], 1.0 / (D * FF), EPS, ALU.mult, ALU.max).then_inc(s_setup_dve, 1)
            dve.wait_ge(s_setup_dve, 3)
            dve.reciprocal(wscale[:], wmean[:]).then_inc(s_setup_dve, 1)
            dve.tensor_scalar(wdeq[:], wmean[:], 1.0 / 127.0, None, ALU.mult).then_inc(s_setup_dve, 1)
            n = 5
            for k, out in enumerate((up_w, down_w)):
                w = raw[:, k * DC * FF:(k + 1) * DC * FF]
                dve.wait_ge(s_setup_dve, n)
                dve.tensor_scalar(w, w, wscale[:, k:k + 1], -1.0, ALU.mult, ALU.max).then_inc(s_setup_dve, 1)
                dve.wait_ge(s_setup_dve, n + 1)
                dve.tensor_scalar(w, w, 1.0, MAGIC, ALU.min, ALU.add).then_inc(s_setup_dve, 1)
                dve.wait_ge(s_setup_dve, n + 2)
                dve.tensor_scalar(out[:].rearrange("p c n -> p (c n)"), w, -MAGIC, None, ALU.add).then_inc(s_setup_dve, 1)
                n += 3
            dve.tensor_copy(gx[:], psW[0][:, P:2 * P])
            dve.tensor_copy(vo[:].rearrange("p c n -> p (c n)"), psW[1][:])
            dve.tensor_copy(identb[:], ident[:])
            dve.tensor_copy(beforeb[:], before).then_inc(s_setup_dve, 3)

            def norm(chain, st, src, out, source_ready, free=None, want=None):
                def stage(t):
                    source_ready(t)
                    dve.bn_stats(st[:, 0:6], src(t)).then_inc(chain.sem, 1)
                    after(dve, chain, t, "stats")
                    carry()
                    dve.bn_aggr(st[:, 6:8], st[:, 0:6]).then_inc(chain.sem, 1)
                    after(dve, chain, t, "mean")
                    dve.tensor_scalar(st[:, 8:9], st[:, 7:8], EPS, None, ALU.add).then_inc(chain.sem, 1)
                    after(dve, chain, t, "rstd")
                    dve.tensor_scalar(out(t), src(t), st[:, 6:7], st[:, 9:10], ALU.subtract, ALU.mult).then_inc(chain.sem, 1)
                return stage

            def a_ready(t):
                dve.wait_ge(in_x[t.par], t.loads())
                after(dve, tail, t.back(1), "x1")

            a_ln = norm(front, stA, lambda t: xa[:, t.par, :], lambda t: xnA[:], a_ready)

            def a_q(t):
                after(dve, front, t, "qT_ps")
                dve.tensor_scalar(qT[:, 4:8, :].rearrange("p j n -> p (j n)"), psW[1][:], DH ** -0.5, None, ALU.mult
                                  ).then_inc(front.sem, 1)

            def a_qp(t, c, g):
                after(dve, front, t, f"qk_ps{2 * c + g}")
                dve.tensor_copy(qk[:, c, :, 8 * g + 1:8 * g + 8:2, :].rearrange("p b h s -> p h b s"),
                                psW[1][:].rearrange("p (h b s) -> p h b s", h=4, b=2)).then_inc(front.sem, 1)

            def a_s(t, u):
                after(dve, scores_ps, t, u)
                dve.tensor_reduce(smA[:, u % 2, 0, :], psS[u % 2][:].rearrange("p (k n) -> p k n", k=2), AX.X, ALU.max,
                                  negate=True).then_inc(neg_max.sem, 1)
                after(dve, exp_done, t, u)
                dve.reciprocal(smA[:, u % 2, 2, :], smA[:, u % 2, 1, :]).then_inc(inv_sum.sem, 1)
                after(dve, inv_sum, t, u)
                for k in range(2):
                    ins = dve.tensor_scalar(prA[:, u % 2, k, :], prA[:, u % 2, k, :], smA[:, u % 2, 2, k:k + 1], None,
                                            ALU.mult)
                ins.then_inc(probs.sem, 1)

            def a_z(t, u):
                b, quarter = divmod(u, 4)
                after(dve, mixed_ps, t, u)
                dve.tensor_copy(zT[:, :, 4 * quarter:4 * quarter + 4, b, :],
                                psW[1][:].rearrange("p (c h s) -> p c h s", c=DC, h=4)).then_inc(mixed.sem, 1)

            def a_v(t):
                after(dve, tail, t, "v_ps")
                dve.tensor_copy(oT[:, 4:8, :].rearrange("p j n -> p (j n)"), psW[1][:]).then_inc(tail.sem, 1)

            def a_y(t):
                after(dve, tail, t, "y_ps")
                after(dve, masked, t.back(2), "biased")
                dve.tensor_tensor(xb[:, t.par, :], psW[0][:, 0:D], xa[:, t.par, :], ALU.add).then_inc(tail.sem, 1)

            def masked_heads(chain, t, wait_for, ps, out):
                after(dve, chain, t, wait_for)
                for m in range(4):
                    dve.tensor_scalar(out[:, :, :, m, :], ps.rearrange("p (c b s) -> p c b s", c=DC, b=2),
                                      head_mask[:, m:m + 1], None, ALU.mult).then_inc(chain.sem, 1)

            def softmax_small(chain, sums, t, scores, pr, sm):
                sc = scores.rearrange("p g (n k) -> p (g n) k", k=S)
                prv = pr[:].rearrange("p g c (b k) -> p (g c b) k", k=S)
                dve.tensor_reduce(sm[:, 0, :], sc, AX.X, ALU.max).then_inc(chain.sem, 1)
                after(dve, chain, t, "max")
                dve.tensor_tensor(prv, sc, wide(sm[:, 0, :], S), ALU.subtract).then_inc(chain.sem, 1)
                after(dve, chain, t, "exp")
                for g in range(2):
                    dve.tensor_reduce(sm[:, 1, :].rearrange("p (c g n) -> p c g n", c=DC, g=2)[:, :, g, :],
                                      pr[:, g].rearrange("p (c s) (b k) -> p c (s b) k", c=DC, k=S), AX.X, ALU.add
                                      ).then_inc(sums.sem, 1)
                after(dve, sums, t, "sum")
                dve.reciprocal(sm[:, 2, :], sm[:, 1, :]).then_inc(sums.sem, 1)

            def second_half_turned(chain, t, ps_step, ps, prT):
                after(dve, chain, t, ps_step)
                dve.tensor_copy(prT[:, 1].rearrange("p c n -> p (c n)"), ps[:, 1, :]).then_inc(chain.sem, 1)

            def heads_small(chain, sums, t, ps, sm, out):
                after(dve, sums, t, "inverse")
                after(dve, chain, t, "out_ps")
                for b in range(2):
                    for half in range(2):
                        rows = slice(S * half, S * half + S)
                        inv = sm[rows, 2, b:16:2].unsqueeze(2).broadcast_to([S, PAIRS, HD])
                        dve.tensor_tensor(
                            out[S * b:S * b + S, :].rearrange("p (j two e) -> p j two e", two=2, e=HD)[:, :, half, :],
                            ps[rows, b, 0:D].rearrange("p (j two e) -> p j two e", two=2, e=HD)[:, :, half, :],
                            inv, ALU.mult).then_inc(chain.sem, 1)

            def add_out(chain, t, ps, x, bias, out):
                after(dve, chain, t, "proj_ps")
                dve.tensor_tensor(out, ps, x, ALU.add).then_inc(chain.sem, 1)
                after(dve, chain, t, "added")
                dve.tensor_tensor(out, out, bias[:], ALU.add).then_inc(chain.sem, 1)

            def b_ready(t):
                after(dve, tail, t, "x1")
                after(dve, masked, t.back(1), "biased")

            xb_of = lambda t: xb[:, t.par, :]
            b_ln = norm(rope, stB, xb_of, lambda t: xnB[:], b_ready)

            def b_qkv(t):
                if t.i is None and t.c == 0:
                    dve.wait_ge(s_zero, 16 * (E * CAP // (4 * P)))
                after(dve, rope, t, "qkv_ps")
                dve.tensor_tensor(qkB[:], psB[:, 0, :], bqkv[:, 0:2 * D], ALU.add).then_inc(rope.sem, 1)
                dve.tensor_tensor(vB[:], psB[:, 1, 0:D], bqkv[:, 2 * D:], ALU.add).then_inc(rope.sem, 1)
                after(dve, rope, t, "qkv")
                dve.tensor_tensor(qcos, qkB[:], rope_cos[:], ALU.mult).then_inc(rope.sem, 1)
                after(dve, rope, t, "turned")
                dve.tensor_tensor(qkB[:], qcos, rot, ALU.add).then_inc(rope.sem, 1)

            def b_qkt(t):
                masked_heads(rope, t, "qkT_ps", psB[:, 0, 0:D], qBB)

            def b_s(t):
                after(dve, rope, t, "scores_ps")
                softmax_small(rope, rope_sums, t, psB[:], prB, smB)

            def b_tr(t):
                second_half_turned(rope, t, "pT_ps", psB, prTB)

            def b_av(t):
                heads_small(rope, rope_sums, t, psB, smB, aoB)

            def b_wo(t):
                add_out(rope, t, psB[:, 1, 0:D], xb_of(t), bo_b, xb_of(t))

            f_norm = norm(ffn, stB, xb_of, lambda t: xnB[:], lambda t: after(dve, rope, t, "biased"))

            def quantise(t, tag, g, n, w):
                step = lambda name: after(dve, ffn, t, tag + name)
                col = lambda k: stB[:, k:k + 1]
                dve.tensor_scalar(col(17), col(16), 1.0 / n, 1e-8, ALU.mult, ALU.add).then_inc(ffn.sem, 1)
                step("rstd")
                dve.tensor_reduce(col(19), g, AX.X, ALU.max, apply_absolute_value=True).then_inc(ffn.sem, 1)
                step("peak")
                dve.tensor_scalar(col(20), col(19), col(18), EPS, ALU.mult, ALU.max).then_inc(ffn.sem, 1)
                step("guarded")
                dve.reciprocal(col(21), col(20)).then_inc(ffn.sem, 1)
                step("inverse")
                dve.tensor_scalar(col(23), col(21), 127.0, col(18), ALU.mult, ALU.mult).then_inc(ffn.sem, 1)
                step("factor")
                dve.tensor_tensor(col(22), col(20), wdeq[:, w:w + 1], ALU.mult).then_inc(ffn.sem, 1)
                step("undo")
                dve.tensor_scalar(g, g, col(23), -128.0, ALU.mult, ALU.max).then_inc(ffn.sem, 1)
                step("clipped")
                dve.tensor_scalar(g, g, 127.0, MAGIC, ALU.min, ALU.add).then_inc(ffn.sem, 1)
                step("rounded")
                dve.tensor_scalar(hq[:, 0:n], g, -MAGIC, None, ALU.add).then_inc(ffn.sem, 1)

            def f_ln(t):
                f_norm(t)
                after(dve, ffn, t, "xn")
                dve.tensor_tensor(hid[:, 0:D], xnB[:], norm1[:], ALU.mult).then_inc(ffn.sem, 1)
                after(dve, ffn, t, "weighed")
                quantise(t, "in_", hid[:, 0:D], D, 0)

            def f_up(t):
                after(dve, ffn, t, "square")
                dve.tensor_scalar(hid[:], hid[:], act_sc[:, 0:1], act_bi[:, 0:1], ALU.mult, ALU.add).then_inc(ffn.sem, 1)
                after(dve, ffn, t, "affine")
                dve.tensor_tensor(g2, hid[:], norm2[:], ALU.mult).then_inc(ffn.sem, 1)
                after(dve, ffn, t, "weighed2")
                quantise(t, "mid_", g2, FF, 1)

            def f_down(t):
                after(dve, ffn, t, "down_ps")
                dve.scalar_tensor_tensor(out=xb_of(t), in0=psB[:, 1, 0:D], scalar=stB[:, 22:23], in1=xb_of(t),
                                         op0=ALU.mult, op1=ALU.add).then_inc(ffn.sem, 1)

            x_ln = norm(masked, stB, xb_of, lambda t: xnB[:], lambda t: after(dve, ffn, t, "added"))

            def x_g(t):
                masked_heads(masked, t, "q_ps", psB[:, 0, 0:D], qBB)

            def x_s(t, b, c):
                u = 2 * b + c
                after(dve, masked, t, f"scores_ps{u}")
                if u == 0:
                    after(dve, mask_ready, t, 0)
                carry()
                for g in range(2):
                    for s in range(2):
                        n = 2 * g + s
                        dve.tensor_tensor_reduce(prB[:, g, 2 * s:2 * s + 2, :].rearrange("p k n -> p (k n)"),
                                                 psB[:, g, s * CTX:(s + 1) * CTX], mask_add[:, b, :], 1.0, -3.0e38,
                                                 ALU.add, ALU.max, smB[:, 0, n:n + 1]).then_inc(masked.sem, 1)
                after(dve, masked, t, f"masked{u}")
                dve.tensor_scalar(smB[:, 1, 0:4], smB[:, 0, 0:4], -(D ** -0.5), None, ALU.mult).then_inc(masked.sem, 1)
                after(dve, masked, t, f"exp{u}")
                dve.reciprocal(smB[:, 2, 4:8], smB[:, 2, 0:4]).then_inc(masked_sums.sem, 1)

            def x_tr(t, b, c):
                second_half_turned(masked, t, f"pT_ps{2 * b + c}", psB, prTB)

            def x_av(t, b, c):
                u = 2 * b + c
                after(dve, masked_sums, t, u)
                after(dve, masked, t, f"out_ps{u}")
                for half in range(2):
                    rows = slice(S * half, S * half + S)
                    cols = slice(4 * c * 2 * HD, 4 * (c + 1) * 2 * HD)
                    dve.tensor_tensor(
                        aoB[S * b:S * b + S, cols].rearrange("p (j two e) -> p j two e", two=2, e=HD)[:, :, half, :],
                        psB[rows, 0, 0:4 * 2 * HD].rearrange("p (j two e) -> p j two e", two=2, e=HD)[:, :, half, :],
                        smB[rows, 2, 4:8].unsqueeze(2).broadcast_to([S, 4, HD]), ALU.mult).then_inc(masked.sem, 1)

            def x_o(t):
                if t.back(2).exists:
                    after(dve, route, t.back(2), "put")
                add_out(masked, t, psB[:, 1, 0:D], xb_of(t), bo_x, xc[:, t.par, :])

            def c_ready(t):
                after(dve, masked, t, "biased")
                after(dve, route, t.back(1), "put")

            xc_of = lambda t: xc[:, t.par, :]
            c_ln = norm(alib, stC, xc_of, lambda t: xnC[:], c_ready)

            def c_qkv(t):
                after(dve, alib, t, "qkv_ps")
                for c in range(DC):
                    for m in range(4):
                        dve.tensor_scalar(qBC[:, c, :, m, :], psC[:, 0, c * P:(c + 1) * P].rearrange("p (b s) -> p b s", b=2),
                                          bqk_c[:, 0, c:c + 1], head_mask[:, m:m + 1], ALU.add, ALU.mult
                                          ).then_inc(alib.sem, 1)
                dve.tensor_tensor(vC[:], psC[:, 0, D:2 * D], bv_c[:], ALU.add).then_inc(alib.sem, 1)

            def c_s(t):
                after(dve, alib, t, "scores_ps")
                for b in range(2):
                    dve.scalar_tensor_tensor(
                        out=prC[:].rearrange("p g c (b k) -> p (g c) b k", b=2)[:, :, b, :],
                        in0=psC[:].rearrange("p g (c b k) -> p (g c) b k", b=2, k=S)[:, :, b, :], scalar=HD ** -0.5,
                        in1=alibi[:].rearrange("p (j k) -> p j k", k=S), op0=ALU.mult, op1=ALU.add).then_inc(alib.sem, 1)
                after(dve, alib, t, "alibi")
                softmax_small(alib, alib_sums, t, prC[:].rearrange("p g c n -> p g (c n)"), prC, smC)

            def c_tr(t):
                second_half_turned(alib, t, "pT_ps", psC, prTC)

            def c_av(t):
                heads_small(alib, alib_sums, t, psC, smC, aoC)

            def c_wo(t):
                add_out(alib, t, psC[:, 1, 0:D], xc_of(t), bo_c, xc_of(t))

            def m_ready(t):
                after(dve, alib, t, "biased")
                if t.back(2).exists:
                    dve.wait_ge(scattered[t.par], t.back(2).landed(TOPK))
                    dve.wait_ge(out_part[t.par], t.back(2).landed(3))

            m_ln = norm(route, stC, xc_of, lambda t: xnM[:, t.par, :], m_ready)

            def m_gu(t):
                step = lambda name: after(dve, route, t, name)
                inc = lambda ins: ins.then_inc(route.sem, 1)
                step("exp")
                inc(dve.tensor_scalar(shared[:, 0, :], shared[:, 0, :], 1.0, None, ALU.add))
                inc(dve.tensor_scalar(gl[:, 0, :], gl[:, 0, :], 1.0, None, ALU.add))
                step("plus1")
                inc(dve.reciprocal(shared[:, 0, :], shared[:, 0, :]))
                inc(dve.reciprocal(gl[:, 1, :], gl[:, 0, :]))
                step("inverse")
                inc(dve.tensor_tensor(shared[:, 0, :], psC[:, 0, 0:P], shared[:, 0, :], ALU.mult))
                inc(dve.tensor_tensor(gl[:, 2, :], gl[:, 1, :], gate_bias[:], ALU.add))
                step("scores")
                inc(dve.tensor_tensor(shared[:, 1, :], psC[:, 0, P:2 * P], shared[:, 0, :], ALU.mult))
                inc(dve.max(top[:], gl[:, 2, :]))
                step("top")
                carry()
                inc(dve.max_index(topi[:], top[:], gl[:, 2, :]))
                step("index")
                inc(dve.tensor_copy(topf[:], topi[:]))
                step("index_f")
                for k in range(TOPK):
                    inc(dve.tensor_scalar(hot[:, k, :], expert_no[:], topf[:, k:k + 1], None, ALU.is_equal))
                step("hot")
                with nc.allow_low_precision(reason="0 and 1 are exact"):
                    inc(dve.tensor_reduce(sel[:], hot[:].rearrange("p k e -> p e k"), AX.X, ALU.add))
                inc(dve.tensor_tensor(hot2[:], hot[:], gl[:, 1, :].unsqueeze(1).broadcast_to([P, TOPK, E]), ALU.mult))
                step("chosen")
                inc(dve.tensor_reduce(rt[:, 0, :], hot2[:], AX.X, ALU.add))
                step("weight")
                inc(dve.tensor_reduce(rt[:, 1, 0:1], rt[:, 0, :], AX.X, ALU.add))
                step("total")
                inc(dve.tensor_scalar(rt[:, 1, 1:2], rt[:, 1, 0:1], 1e-12, None, ALU.max))
                step("guarded")
                inc(dve.reciprocal(rt[:, 1, 2:3], rt[:, 1, 1:2]))
                step("over_total")
                inc(dve.tensor_scalar(rt[:, 2, :], rt[:, 0, :], rt[:, 1, 2:3], None, ALU.mult))

            def m_out(t):
                step = lambda name: after(dve, route, t, name)
                inc = lambda ins: ins.then_inc(route.sem, 1)
                p = t.par
                step("pos_ps")
                inc(dve.tensor_tensor(hot2[:], hot[:], psC[:, 1, 0:E].unsqueeze(1).broadcast_to([P, TOPK, E]), ALU.mult))
                inc(dve.tensor_tensor(part[:, p, :], psC[:, 0, 0:D], xc_of(t), ALU.add))
                step("hot_pos")
                inc(dve.tensor_reduce(rt[:, 3, :], hot2[:], AX.X, ALU.add))
                step("pos")
                inc(dve.tensor_tensor(seen[:], seen[:], sel[:], ALU.add))
                inc(dve.tensor_scalar(rt[:, 4, :], rt[:, 3, :], float(CAP), None, ALU.is_lt))
                inc(dve.tensor_scalar(rt[:, 5, :], rt[:, 3, :], float(CAP), FAR, ALU.is_ge, ALU.mult))
                inc(dve.tensor_scalar(rt[:, 6, :], topf[:, 0:TOPK], float(CAP), None, ALU.mult))
                inc(dve.tensor_scalar(rt[:, 7, :], rt[:, 3, :], float(CAP - 1), None, ALU.min))
                step("limits")
                inc(dve.tensor_tensor(gate[:, p, :], rt[:, 2, :], rt[:, 4, :], ALU.mult))
                inc(dve.tensor_tensor(slot[:, p, :], rt[:, 6, :], rt[:, 7, :], ALU.add))
                inc(dve.tensor_tensor(rt[:, 8, :], rt[:, 6, :], rt[:, 5, :], ALU.add))
                step("places")
                inc(dve.tensor_tensor(put[:, p, :], rt[:, 8, :], rt[:, 3, :], ALU.add))

            run(dve, {k: v for k, v in locals().items() if k in STAGE_NAMES})

            def expert(e):
                after(dve, ex, e, "exp")
                dve.tensor_scalar(ex_h[:, 0, :], ex_h[:, 0, :], 1.0, None, ALU.add).then_inc(ex.sem, 1)
                after(dve, ex, e, "plus1")
                dve.reciprocal(ex_h[:, 0, :], ex_h[:, 0, :]).then_inc(ex.sem, 1)
                after(dve, ex, e, "inverse")
                dve.tensor_tensor(ex_h[:, 0, :], psB[:, 1, 0:CAP], ex_h[:, 0, :], ALU.mult).then_inc(ex.sem, 1)
                after(dve, ex, e, "silu")
                dve.tensor_tensor(ex_h[:, 1, :], psB[:, 1, CAP:2 * CAP], ex_h[:, 0, :], ALU.mult).then_inc(ex.sem, 1)

            expert(Tile(0))
            expert(Tile(1))
            with dve.Fori(0, (E - 2) // 2) as i:
                expert(Tile(2, i))
                expert(Tile(3, i))

            def add_rows(t):
                p = t.par
                dve.wait_ge(sum_in[p], t.landed(3))
                dve.wait_ge(sum_rows[p], t.landed(TOPK))
                for k in range(TOPK):
                    if k or t.back(1).exists:
                        dve.wait_ge(summed.sem, t.count(TOPK, k))
                    dve.scalar_tensor_tensor(out=fin[:, p, :], in0=fin_rows[:, p, k, :], scalar=fin_gate[:, p, k:k + 1],
                                             in1=fin[:, p, :], op0=ALU.mult, op1=ALU.add).then_inc(summed.sem, 1)

            add_rows(Tile(0))
            add_rows(Tile(1))
            with dve.Fori(0, (TILES - 2) // 2) as i:
                add_rows(Tile(2, i))
                add_rows(Tile(3, i))


_T = ["L0_xattn_Wk", "L0_ffn_w1", "L0_ffn_w2", "L1_xattn_Wo", "L1_ffn_gate_w", "L1_ffn_sw1", "L1_ffn_sw3", "L1_ffn_sw2"]


def constants():
    p = np.arange(P)
    f = np.float32
    c = {"c_ident": np.eye(P, dtype=f),
         "c_head_mask": ((p[:, None] % S) // HD == np.arange(4)[None, :]).astype(f),
         "c_before": (p[:, None] < p[None, :]).astype(f),
         "c_expert_no": np.tile(np.arange(E, dtype=f), (P, 1))}
    inv_freq = f(1.0) / np.power(f(10000.0), np.arange(0, HD, 2, dtype=f) / f(HD))
    ang = (p % S).astype(f)[:, None] * inv_freq[None, :]
    sin, cos = np.sin(ang), np.cos(ang)
    c["c_rope_cos"] = np.tile(np.concatenate([cos, cos], 1), (1, 2 * H)).astype(f)
    c["c_rope_sin"] = np.tile(np.concatenate([-sin, sin], 1), (1, 2 * H)).astype(f)
    slopes = f(1.0) / np.power(f(2.0), np.arange(H, dtype=f) / f(H))
    g, cc, s = np.meshgrid(np.arange(2), np.arange(2), np.arange(2), indexing="ij")
    head = 2 * (4 * cc + 2 * g + s).reshape(-1)[None, :] + (p // S)[:, None]
    rel = np.arange(S, dtype=f)[None, :] - (p % S).astype(f)[:, None]
    c["c_alibi"] = (slopes[head][:, :, None] * rel[:, None, :]).reshape(P, -1).astype(f)
    return c


def kernel(**inputs):
    import concourse.bacc as bacc
    from concourse.bass_utils import run_bass_kernel_spmd

    arrays = {}
    for name, v in inputs.items():
        v = np.asarray(v)
        if name == "x":
            v = v.reshape(-1, D)
        elif name == "ctx_1024":
            arrays["ctx"] = np.ascontiguousarray(v)
            arrays["ctxT"] = np.ascontiguousarray(v.transpose(0, 2, 1))
            continue
        elif name == "mask_Bx1xSxS2_ik1":
            name, v = "mask", v[:, 0]
        elif name in _T:
            name, v = name + "T", v.T
        elif name in ("L1_ffn_W1", "L1_ffn_W3", "L1_ffn_W2"):
            v = v.reshape(-1, v.shape[-1])
        elif name in ("L1_attn_bq", "L1_attn_bk"):
            v = v.reshape(DC, P).T
        arrays[name] = np.ascontiguousarray(v)
    arrays.update(constants())

    nc = bacc.Bacc("TRN2", target_bir_lowering=False, num_devices=1)
    a = {n: nc.dram_tensor("in_" + n, v.shape, mybir.dt.from_np(v.dtype), kind="ExternalInput").ap()
         for n, v in arrays.items()}
    a["out"] = nc.dram_tensor("out_x", arrays["x"].shape, F32, kind="ExternalOutput").ap()
    build(nc, a)
    r = run_bass_kernel_spmd(nc, [{"in_" + n: v for n, v in arrays.items()}], core_ids=[0])
    return np.asarray(r.results[0]["out_x"]).reshape(np.shape(inputs["x"]))
```

```python
from contextlib import ExitStack

import numpy as np

import concourse.bass as bass
from concourse import mybir

F32 = mybir.dt.float32
BF16 = mybir.dt.bfloat16
I32 = mybir.dt.int32
U32 = mybir.dt.uint32
ALU = mybir.AluOpType
ACT = mybir.ActivationFunctionType
AX = mybir.AxisListType

P = 128
S = 64
D = 256
DC = D // P
CTX = 256
KC = CTX // P
H = 16
PAIRS = H // 2
DH = 64
HD = D // H
FF = 1024
E = 32
TOPK = 4
EI = 128
CAP = 2 * (2 * 512) * TOPK // E
EPS = 1e-5
MAGIC = 12582912.0
FAR = float(1 << 20)
UNITS = 8


class Tile:

    def __init__(self, c, i=None):
        self.c, self.i = c, i
        self.par = c % 2

    def back(self, n):
        return Tile(self.c - n, self.i)

    @property
    def exists(self):
        return self.i is not None or self.c >= 0

    def count(self, per_tile, k):
        v = self.c * per_tile + k
        return v if self.i is None else self.i * (2 * per_tile) + v

    def loads(self):
        v = 16 * (self.c // 2 + 1)
        return v if self.i is None else self.i * 16 + v

    def landed(self, n):
        return self.loads() * n if self.i is None else self.i * (16 * n) + 16 * n * (self.c // 2 + 1)

    def row(self):
        return self.c if self.i is None else self.i * 2 + self.c


class Chain:

    def __init__(self, sem, steps):
        self.sem, self.index, n = sem, {}, 0
        for step in steps:
            name, k = step if isinstance(step, tuple) else (step, 1)
            assert name not in self.index, name
            n += k
            self.index[name] = n
        self.per_tile = n

    def at(self, tile, step):
        return tile.count(self.per_tile, self.index[step])


class Signal:

    def __init__(self, sem, per_tile):
        self.sem, self.per_tile = sem, per_tile

    def at(self, tile, k):
        return tile.count(self.per_tile, k + 1)


NORM = ["stats", "mean", "var", "rstd", "xn", "xnT_ps", "xnT"]
QKV_A = [("qT_ps", 1), ("qT", 2)] + [x for n in range(4) for x in (f"qk_ps{n}", (f"qk{n}", 2))]
SOFTMAX = ["shifted", "exp", "pT_ps", ("pT", 2), "out_ps", ("heads", 4),
           "headsT_ps", "headsT", "proj_ps", "added", "biased"]
ROPE_ATTN = NORM + ["qkv_ps", ("qkv", 2), ("turned", 3), "roped", "qkT_ps", ("qkT", 5),
                    "scores_ps", "max"] + SOFTMAX
QUANT = [("var", 1), ("rstd", 2), ("guarded", 1), ("inverse", 2), ("factor", 1), ("clipped", 1), ("rounded", 1), ("quant", 1)]
FFN = (NORM[:5] + [("weighed", 2)] + [("in_" + name, n) for name, n in QUANT]
       + ["inT_ps", "inT", "up_ps", ("relu", 2), "square", "affine", ("weighed2", 2)]
       + [("mid_" + name, n) for name, n in QUANT] + ["midT_ps", "midT", "down_ps", "added"])
MASKED = NORM + ["q_ps", ("q", 4)]
MASKED_OUT = ["headsT_ps", "headsT", "proj_ps", "added", "biased"]
ALIBI_ATTN = NORM + ["qkv_ps", ("qkv", 11), "scores_ps", ("alibi", 2), "max"] + SOFTMAX
ROUTE = (NORM + ["up_ps", ("exp", 2), ("plus1", 2), ("inverse", 2), ("scores", 2), ("top", 2), "index", "index_f",
                 ("hot", 4), ("chosen", 2), "weight", "total", "guarded", "over_total", "gates", "pos_ps",
                 ("hot_pos", 2), "pos", ("limits", 5), ("places", 3), "put"])

N_STAGES = ["a_ln", "a_nx"]
A_STAGES = (["a_xt", "a_q"] + [("a_qp", c, g) for c in range(DC) for g in range(2)]
            + [("a_s", 0), ("a_s", 1), ("a_n", 0)]
            + [x for u in range(UNITS)
               for x in ([("a_tr", u)] + ([("a_n", u + 1)] if u + 1 < UNITS else [])
                         + ([("a_s", u + 2)] if u + 2 < UNITS else []) + [("a_z", u)])]
            + ["a_v", "a_y"])
B_STAGES = ["b_ln", "b_nx", "b_xt", "b_qkv", "b_ro", "b_qkt", "b_s", "b_tr", "b_n", "b_av", "b_aot", "b_wo",
            "f_ln", "f_nx", "f_q1", "f_q2", "f_xt", "f_up", "f_w", "f_q3", "f_q4", "f_q5", "f_ht", "f_down"]
D_STAGES = (["d_ln", "d_nx", "d_xt", "d_g", ("d_s", 0)]
            + [x for u in range(UNITS)
               for x in ([("d_s", u + 1)] if u + 1 < UNITS else []) + [("d_tr", u), ("d_av", u)]]
            + ["d_zt", "d_o"])
C_STAGES = ["c_ln", "c_nx", "c_xt", "c_qkv", "c_s", "c_tr", "c_n", "c_av", "c_aot", "c_wo",
            "m_ln", "m_nx", "m_xt", "m_gu", "m_g1", "m_g2", "m_g3", "m_out", "m_put"]
SPAN = {"a_ln": 2, "a_q": 2, "a_qp": 2, "a_s": 2, "a_z": 2, "a_v": 2, "a_y": 2,
        "b_ln": 2, "b_qkv": 1.5, "b_qkt": 3, "b_s": 7, "b_tr": 2, "b_av": 3, "b_wo": 2,
        "f_nx": 2, "f_q2": 3, "f_q5": 2, "f_up": 5, "f_q3": 4, "f_q4": 4, "f_ht": 2, "f_down": 2,
        "d_ln": 2, "d_g": 2, "d_tr": 2, "d_s": 2,
        "c_ln": 2, "c_qkv": 4, "c_s": 6, "c_tr": 2, "c_av": 3, "c_wo": 2, "c_aot": 0.7,
        "m_ln": 2.8, "m_gu": 2, "m_g1": 2, "m_g2": 4, "m_g3": 3, "m_out": 2, "m_put": 2, "m_xt": 1.4}
STAGE_NAMES = {s[0] if isinstance(s, tuple) else s for s in N_STAGES + A_STAGES + B_STAGES + D_STAGES + C_STAGES}


START = {"N": -0.15, "A": 0.0, "B": 1.0, "D": 2.05, "C": 3.15}


def merged(**streams):
    keyed = []
    for name, stages in streams.items():
        spans = [SPAN.get(s[0] if isinstance(s, tuple) else s, 1) for s in stages]
        length = sum(spans) / (0.1 if name == "N" else 1.0)
        at = START[name] * length
        for s, span in zip(stages, spans):
            time = (at + 0.5) / length
            behind = int(np.floor(time))
            keyed.append((time - behind, len(keyed), behind, s))
            at += span
    return [(behind, s) for _, _, behind, s in sorted(keyed, key=lambda x: x[:2])]


def build(nc, a):
    TILES = a["x"].shape[0] // P
    assert TILES % 2 == 0 and TILES >= 10

    ctx = ExitStack()
    with ctx:
        def sb(name, shape, dt=F32):
            return ctx.enter_context(nc.sbuf_tensor(name, shape, dt))

        def sem(name):
            return ctx.enter_context(nc.semaphore(name))

        def scratch(name, shape, dt=F32):
            return nc.dram_tensor(name, shape, dt, kind="Internal").ap()

        expert_in = scratch("expert_in", (E * CAP, D))
        places = scratch("places", (E * CAP, 2), I32)

        psS = [ctx.enter_context(nc.psum_tensor(f"psS{n}", [P, 512], F32)) for n in range(2)]
        psW = ctx.enter_context(nc.psum_tensor("psW", [P, 512], F32))
        psB = ctx.enter_context(nc.psum_tensor("psB", [P, 2, 512], F32))
        psD = ctx.enter_context(nc.psum_tensor("psD", [P, 512], F32))
        psC = ctx.enter_context(nc.psum_tensor("psC", [P, 2, 512], F32))

        class Area:

            def __init__(self, buffer):
                self.buffer, self.at = buffer, 0

            def cut(self, *shape, dt=F32):
                n = int(np.prod(shape)) * (2 if dt == BF16 else 4) // 4
                piece = self.buffer[:, self.at:self.at + n]
                self.at += n
                if dt != F32:
                    piece = piece.bitcast(dt)
                dims = "abcd"[:len(shape)]
                if len(shape) == 1:
                    return piece
                return piece.rearrange(f"p ({' '.join(dims)}) -> p {' '.join(dims)}",
                                       **{k: v for k, v in zip(dims, shape)})

        qk = sb("qk", [P, DC, 2, H, S])
        raw = qk[:].rearrange("p c b h s -> p (c b h s)")
        area_c = sb("area_c", [P, 2048])
        cx = sb("cx", [P, 2, 2 * KC, D])
        cxT = sb("cxT", [P, 2, DC, 2, CTX])
        setup = Area(area_c)

        once = []

        def const(name, shape, src, dt=F32):
            t = sb(name, shape, dt)
            once.append((t[:], src))
            return t

        def const_for_setup(shape, src, dt=F32):
            t = setup.cut(*shape, dt=dt)
            once.append((t, src))
            return t

        def spread(v, n):
            return v.rearrange("(a n) -> a n", a=1).broadcast_to([P, n])

        def chunked(w):
            return w.rearrange("(c p) n -> p c n", p=P)

        ident = const("ident", [P, P], a["c_ident"])
        head_mask = const("head_mask", [P, 4], a["c_head_mask"])
        before = const_for_setup([P], a["c_before"])
        expert_no = const("expert_no", [P, E], a["c_expert_no"])
        rope_cos = const("rope_cos", [P, 2 * D], a["c_rope_cos"])
        rope_sin = const("rope_sin", [P, 2 * D], a["c_rope_sin"])
        alibi = const("alibi", [P, PAIRS * S], a["c_alibi"])
        wq = const("wq", [P, DC, H * DH], chunked(a["L0_xattn_Wq"]))
        wkT = const("wkT", [P, PAIRS, D], chunked(a["L0_xattn_WkT"]))
        wv = const("wv", [P, DC, H * DH], chunked(a["L0_xattn_Wv"]))
        wo = const("wo", [P, PAIRS, D], chunked(a["L0_xattn_Wo"]))
        bqkv = sb("bqkv", [P, 3 * D])
        wqkv_b = sb("wqkv_b", [P, DC, 3 * D])
        for n, k in enumerate("qkv"):
            once.append((wqkv_b[:, :, n * D:(n + 1) * D], chunked(a["L0_attn_w" + k])))
            once.append((bqkv[:, n * D:(n + 1) * D], spread(a["L0_attn_b" + k], D)))
        wo_b = const("wo_b", [P, DC, D], chunked(a["L0_attn_wo"]))
        bo_b = const("bo_b", [P, D], spread(a["L0_attn_bo"], D))
        norm1 = const("norm1", [P, D], spread(a["L0_ffn_norm1_w"], D))
        norm2 = const("norm2", [P, FF], spread(a["L0_ffn_norm2_w"], FF))
        act_sc = const("act_sc", [P, 1], spread(a["L0_ffn_act_scale"], 1))
        act_bi = const("act_bi", [P, 1], spread(a["L0_ffn_act_bias"], 1))
        woT_x = const_for_setup([DC, D], chunked(a["L1_xattn_WoT"]))
        bo_x = const("bo_x", [P, D], spread(a["L1_xattn_bo"], D))
        w_c = sb("w_c", [P, DC, 3 * D])
        for n, k in enumerate("qkv"):
            once.append((w_c[:, :, n * D:(n + 1) * D], chunked(a["L1_attn_W" + k])))
        bqk_c = sb("bqk_c", [P, 2, DC])
        for n, k in enumerate("qk"):
            once.append((bqk_c[:, n, :], a["L1_attn_b" + k]))
        bv_c = const("bv_c", [P, D], spread(a["L1_attn_bv"], D))
        wo_c = const("wo_c", [P, DC, D], chunked(a["L1_attn_Wo"]))
        bo_c = const("bo_c", [P, D], spread(a["L1_attn_bo"], D))
        gate_bias = const("gate_bias", [P, E], spread(a["L1_ffn_bias"], E))
        gate_bf = const_for_setup([DC, E], chunked(a["L1_ffn_gate_wT"]), BF16)
        sw13_bf = setup.cut(DC, 2 * EI, dt=BF16)
        once.append((sw13_bf[:, :, 0:EI], chunked(a["L1_ffn_sw1T"])))
        once.append((sw13_bf[:, :, EI:2 * EI], chunked(a["L1_ffn_sw3T"])))
        sw2_bf = const_for_setup([D], a["L1_ffn_sw2T"], BF16)
        diag = setup.cut(3, P)
        diag_loads = [(diag[HD * h:HD * h + HD, n, HD * h:HD * h + HD], a["L1_xattn_W" + k])
                      for n, k in enumerate("qkv") for h in range(P // HD)]

        identb = sb("identb", [P, P], BF16)
        beforeb = sb("beforeb", [P, P], BF16)
        onesb = sb("onesb", [P, P], BF16)
        ones = sb("ones", [P, P])
        neg_half = sb("neg_half", [P, 1])
        carrier = sb("carrier", [P, 2])
        up_w = sb("up_w", [P, DC, FF], BF16)
        down_w = sb("down_w", [P, FF // P, D], BF16)
        wsum = sb("wsum", [P, 2])
        wmean = sb("wmean", [P, 2])
        wscale = sb("wscale", [P, 2])
        wdeq = sb("wdeq", [P, 2])
        gx = sb("gx", [P, P])
        vo = sb("vo", [P, DC, D])
        gate_w = sb("gate_w", [P, DC, E])
        sw13 = sb("sw13", [P, DC, 2 * EI])
        sw2 = sb("sw2", [P, D])
        
        xa = sb("xa", [P, 2, D])
        xnA, xnTA = sb("xnA", [P, D]), sb("xnTA", [P, DC, P])
        stA = sb("stA", [P, 16])
        prTA = sb("prTA", [P, 2, KC, 2 * P])
        qT = prTA[:].rearrange("p u k n -> p (u k n)").rearrange("p (j n) -> p j n", j=PAIRS)
        oT = qT
        prA = sb("prA", [P, 2, 2, CTX])
        smA = sb("smA", [P, 2, 3, 2])
        up_raw = raw[:, 0:DC * FF].rearrange("p (c n) -> p c n", c=DC)
        down_raw = raw[:, DC * FF:2 * DC * FF].rearrange("p (c n) -> p c n", n=D)
        once.append((up_raw, chunked(a["L0_ffn_w1T"])))
        once.append((down_raw, chunked(a["L0_ffn_w2T"])))
        xb = sb("xb", [P, 2, D])
        xnB, xnTB = sb("xnB", [P, D]), sb("xnTB", [P, DC, P])
        stB = sb("stB", [P, 32])
        qkB = sb("qkB", [P, 2 * D])
        vB = sb("vB", [P, D])
        kTB = sb("kTB", [P, DC, P])
        prB = sb("prB", [P, 2, 4, 2 * S])
        smB = sb("smB", [P, 3, 16])
        aoB, aoTB = sb("aoB", [P, D]), sb("aoTB", [P, DC, P])
        hid = sb("hid", [P, FF])
        hq = sb("hq", [P, FF], BF16)
        sq = sb("sq", [P, FF])
        hqT = sb("hqT", [P, FF // P, P], BF16)
        qcos, rot = hid[:, 0:2 * D], sq[:, 0:2 * D]
        qBB = sq[:].rearrange("p (c b m s) -> p c b m s", c=DC, b=2, m=4)
        prTB = hid[:].rearrange("p (g c n) -> p g c n", g=2, c=4)
        g2 = prB[:].rearrange("p g c n -> p (g c n)")
        xd = sb("xd", [P, 2, D])
        cxD = sb("cxD", [P, 2 * KC, D])
        cxTD = sb("cxTD", [P, DC, 2, CTX])
        mask = sb("mask", [P, 2, CTX], I32)
        mask_add = sb("mask_add", [P, 2, CTX])
        xnD, xnTD = sb("xnD", [P, D]), sb("xnTD", [P, DC, P])
        stD = sb("stD", [P, 16])
        qBD = sb("qBD", [P, DC, 2, 4, S])
        prD = sb("prD", [P, 2, 2, CTX])
        smD = sb("smD", [P, 2, 3, 2])
        prTD = sb("prTD", [P, 2, KC, P])
        aoD, aoTD = sb("aoD", [P, D]), sb("aoTD", [P, DC, P])
        xc = sb("xc", [P, 2, D])
        xnC, xnTC = sb("xnC", [P, D]), sb("xnTC", [P, DC, P])
        xnM = sb("xnM", [P, 2, D])
        stC = sb("stC", [P, 16])
        vC = sb("vC", [P, D])
        kTC = sb("kTC", [P, DC, P])
        qBC = area_c[:, 0:1024].rearrange("p (c b m s) -> p c b m s", c=DC, b=2, m=4)
        prC = area_c[:, 1024:2048].rearrange("p (g c n) -> p g c n", g=2, c=4)
        smC = sb("smC", [P, 3, 16])
        prTC = sb("prTC", [P, 2, 4, P])
        aoC, aoTC = sb("aoC", [P, D]), sb("aoTC", [P, DC, P])
        shared = sb("shared", [P, 2, P])
        gl = sb("gl", [P, 3, E])
        top = sb("top", [P, 8])
        topi = sb("topi", [P, 8], U32)
        topf = sb("topf", [P, 8])
        hot = sb("hot", [P, TOPK, E])
        hot2 = sb("hot2", [P, TOPK, E])
        sel = sb("sel", [P, E], BF16)
        seen = sb("seen", [P, E], BF16)
        rt = sb("rt", [P, 8, TOPK])
        token = const("token", [P, 1], a["c_token"])
        row_meta = sb("row_meta", [P, 2, TOPK, 2], I32)
        put = sb("put", [P, 2, TOPK], I32)
        part = sb("part", [P, 2, D])

        s_once, s_diag, s_zero = sem("s_once"), sem("s_diag"), sem("s_zero")
        s_tables = sem("s_tables")
        s_setup_dve, s_setup_act = sem("s_setup_dve"), sem("s_setup_act")
        s_setup_pe, s_setup_pool = sem("s_setup_pe"), sem("s_setup_pool")
        in_x = [sem(f"in_x{n}") for n in range(2)]
        in_cx = [sem(f"in_cx{n}") for n in range(2)]
        in_mask, in_cxD = sem("in_mask"), sem("in_cxD")
        out_part = [sem(f"out_part{n}") for n in range(2)]
        scattered = [sem(f"scattered{n}") for n in range(2)]
        late = Area(raw)
        ex_x, ex_y = late.cut(2, KC, D), late.cut(2, KC, D)
        ex_xT, ex_h = late.cut(2, DC, CAP), late.cut(2, 2, CAP)
        late = Area(cx[:].rearrange("p u k d -> p (u k d)"))
        ex_w13, ex_w2 = late.cut(2, DC, 2 * EI, dt=BF16), late.cut(2, D, dt=BF16)
        ex_meta = late.cut(2, KC, 2, dt=I32)
        ex_w13f = late.cut(DC, 2 * EI)
        late = Area(cxT[:].rearrange("p u c b k -> p (u c b k)"))
        ex_w2f = late.cut(2, D)

        front = Chain(sem("front"), NORM + QKV_A)
        tail = Chain(sem("tail"), ["v_ps", ("oT", 2), "y_ps", "x1"])
        scores_ps = Signal(sem("scores_ps"), UNITS)
        neg_max = Signal(sem("neg_max"), UNITS)
        exp_done = Signal(sem("exp_done"), UNITS)
        inv_sum = Signal(sem("inv_sum"), UNITS)
        probs = Signal(sem("probs"), UNITS)
        probsT_ps = Signal(sem("probsT_ps"), UNITS)
        probsT = Signal(sem("probsT"), UNITS)
        mixed_ps = Signal(sem("mixed_ps"), UNITS)
        mixed = Signal(sem("mixed"), UNITS)
        rope = Chain(sem("rope"), ROPE_ATTN)
        rope_sums = Chain(sem("rope_sums"), [("sum", 2), "inverse"])
        alib_sums = Chain(sem("alib_sums"), [("sum", 2), "inverse"])
        ffn = Chain(sem("ffn"), FFN)
        masked = Chain(sem("masked"), MASKED)
        masked_out = Chain(sem("masked_out"), MASKED_OUT)
        m_scores_ps = Signal(sem("m_scores_ps"), UNITS)
        m_masked = Signal(sem("m_masked"), UNITS)
        m_exp = Signal(sem("m_exp"), UNITS)
        m_inverse = Signal(sem("m_inverse"), UNITS)
        m_probsT_ps = Signal(sem("m_probsT_ps"), UNITS)
        m_probsT = Signal(sem("m_probsT"), UNITS)
        m_out_ps = Signal(sem("m_out_ps"), UNITS)
        m_heads = Signal(sem("m_heads"), UNITS)
        mask_ready = Signal(sem("mask_ready"), 1)
        alib = Chain(sem("alib"), ALIBI_ATTN)
        route = Chain(sem("route"), ROUTE)
        ex_in = [sem(f"ex_in{n}") for n in range(2)]
        ex_meta_in = [sem(f"ex_meta_in{n}") for n in range(2)]
        ex_weights = Signal(sem("ex_weights"), 1)
        ex_xT_ps, ex_xT_in = Signal(sem("ex_xT_ps"), 1), Signal(sem("ex_xT_in"), 1)
        ex_up_ps, ex_exp = Signal(sem("ex_up_ps"), 1), Signal(sem("ex_exp"), 1)
        ex_act = Chain(sem("ex_act"), ["plus1", "inverse", "silu", "h"])
        ex_down_ps, ex_rows = Signal(sem("ex_down_ps"), 1), Signal(sem("ex_rows"), 1)
        ex_added = sem("ex_added")

        block = ctx.enter_context(nc.Block())
        ORDER = merged(N=N_STAGES, A=A_STAGES, B=B_STAGES, D=D_STAGES, C=C_STAGES)

        def added(e):
            return e.count(16 * KC, 16 * KC)

        def run(eng, stages, extra=None):
            def body(t):
                for behind, stage in ORDER:
                    name, args = (stage[0], stage[1:]) if isinstance(stage, tuple) else (stage, ())
                    tile = t.back(behind)
                    if name in stages and tile.exists and (tile.i is not None or tile.c < TILES):
                        stages[name](tile, *args)
                if extra is not None:
                    extra(t)
            for c in range(-1, 6):
                body(Tile(c))
            with eng.Fori(0, (TILES - 8) // 2) as i:
                body(Tile(6, i))
                body(Tile(7, i))
            for c in range(TILES - 2, TILES + 5):
                body(Tile(c))

        def unit(u):
            return u // 4, u // 2 % 2, u % 2

        def skewed(eng, *parts):
            def rnd(e):
                for f, lag in parts:
                    x = e.back(lag)
                    if x.exists and (x.i is not None or x.c < E):
                        f(x)
            for c in range(4):
                rnd(Tile(c))
            with eng.Fori(0, (E - 4) // 2) as i:
                rnd(Tile(4, i))
                rnd(Tile(5, i))
            for c in range(E, E + max(lag for _, lag in parts)):
                rnd(Tile(c))

        @block.sync
        def _(sp):
            for dst, src in once:
                sp.dma_start(dst, src).then_inc(s_once, 16)
            sp.wait_ge(s_setup_pool, 2)
            for dst, src in diag_loads:
                sp.dma_start(dst, src).then_inc(s_diag, 16)

            sp.dma_start(places[:, :], a["c_places"]).then_inc(s_tables, 16)
            sp.dma_start(a["out"][TILES * P:, :], a["c_zero_rows"]).then_inc(s_tables, 16)

            def load(t):
                p = t.par
                samples = bass.ts(t.row(), 2)
                if t.back(2).exists:
                    sp.wait_ge(tail.sem, tail.at(t.back(2), "x1"))
                sp.dma_start(xa[:, p, :], a["x"][bass.ts(t.row(), P), :]).then_inc(in_x[p], 16)
                sp.dma_start(cx[:, p], a["ctx"][samples].rearrange("b (k p) d -> p (b k) d", p=P)).then_inc(in_cx[p], 16)
                for b in range(2):
                    sp.dma_start(cxT[:, p, :, b, :], a["ctxT"][t.row() * 2 + b].rearrange("(c p) k -> p c k", p=P)
                                 ).then_inc(in_cx[p], 16)

            def load_masked(t):
                samples = bass.ts(t.row(), 2)
                if t.back(1).exists:
                    sp.wait_ge(mask_ready.sem, mask_ready.at(t.back(1), 0))
                for half in range(2):
                    sp.dma_start(mask[S * half:S * half + S], a["mask"][samples].rearrange("b q k -> q b k")
                                 ).then_inc(in_mask, 16)
                if t.back(1).exists:
                    sp.wait_ge(m_out_ps.sem, m_out_ps.at(t.back(1), UNITS - 1))
                sp.dma_start(cxD[:], a["ctx"][samples].rearrange("b (k p) d -> p (b k) d", p=P)).then_inc(in_cxD, 16)
                for b in range(2):
                    sp.dma_start(cxTD[:, :, b, :], a["ctxT"][t.row() * 2 + b].rearrange("(c p) k -> p c k", p=P)
                                 ).then_inc(in_cxD, 16)

            def store(t):
                sp.wait_ge(route.sem, route.at(t, "put"))
                sp.dma_start(a["out"][bass.ts(t.row(), P), :], part[:, t.par, :]).then_inc(out_part[t.par], 16)

            def traffic(t):
                if t.exists and (t.i is not None or t.c < TILES):
                    load(t)
                masked_tile, stored = t.back(2), t.back(5)
                if masked_tile.exists and (t.i is not None or masked_tile.c < TILES):
                    load_masked(masked_tile)
                if stored.exists and (t.i is not None or stored.c < TILES):
                    store(stored)

            run(sp, {}, traffic)

            for p in range(2):
                sp.wait_ge(scattered[p], 16 * 2 * TOPK * (TILES // 2))

            def load_expert(e):
                p = e.par
                r = e.row()
                if e.back(2).exists:
                    sp.wait_ge(ex_xT_ps.sem, ex_xT_ps.at(e.back(2), 0))
                sp.dma_start(ex_x[:, p], expert_in[bass.ts(r, CAP), :].rearrange("(k p) d -> p k d", p=P)
                             ).then_inc(ex_in[p], 16)
                if e.back(2).exists:
                    sp.wait_ge(ex_weights.sem, ex_weights.at(e.back(2), 0))
                sp.dma_start(ex_w13[:, p, :, 0:EI], a["L1_ffn_W1"][bass.ts(r, D), :].rearrange("(c p) n -> p c n", p=P)
                             ).then_inc(ex_in[p], 16)
                sp.dma_start(ex_w13[:, p, :, EI:], a["L1_ffn_W3"][bass.ts(r, D), :].rearrange("(c p) n -> p c n", p=P)
                             ).then_inc(ex_in[p], 16)
                sp.dma_start(ex_w2[:, p], a["L1_ffn_W2"][bass.ts(r, EI), :]).then_inc(ex_in[p], 16)

            load_expert(Tile(0))
            load_expert(Tile(1))
            with sp.Fori(0, (E - 2) // 2) as i:
                for c in (2, 3):
                    load_expert(Tile(c, i))
            sp.wait_ge(ex_added, 16 * KC * E)

        @block.tensor
        def _(pe):
            def mm(out, lhsT, rhs, first, last, **kw):
                return pe.matmul(out, lhsT, rhs, start=first, stop=last, **kw)

            pe.wait_ge(s_once, 16 * len(once))
            pe.wait_ge(s_diag, 16 * len(diag_loads))
            pe.wait_ge(s_setup_pool, 7)
            pe.wait_ge(s_setup_dve, 2)
            mm(psW[:, 0:2], ones[:], wsum[:], True, True)
            mm(psW[:, P:2 * P], diag[:, 0, :], diag[:, 1, :], True, True).then_inc(s_setup_pe, 1)
            for c in range(DC):
                ins = mm(psS[0][:, c * D:(c + 1) * D], diag[:, 2, :], woT_x[:, c, :], True, True)
            ins.then_inc(s_setup_pe, 1)
            pe.wait_ge(s_setup_dve, 14)
            pe.wait_ge(s_setup_act, 3)

            def turn(out, src, n=DC):
                for c in range(n):
                    ins = pe.transpose(out[:, c * P:(c + 1) * P], src[:, c * P:(c + 1) * P], ident[:])
                return ins

            def project(out, lhsT, rhs):
                for c in range(DC):
                    ins = mm(out, lhsT[:, c, :], rhs[:, c, :], c == 0, c == DC - 1)
                return ins

            def a_xt(t):
                pe.wait_ge(front.sem, front.at(t, "xn"))
                if t.back(1).exists:
                    pe.wait_ge(tail.sem, tail.at(t.back(1), "x1"))
                turn(psW[:, 0:D], xnA[:]).then_inc(front.sem, 1)

            def a_q(t):
                pe.wait_ge(front.sem, front.at(t, "xnT"))
                for j in range(PAIRS):
                    ins = project(psS[j // 4][:, (j % 4) * P:(j % 4 + 1) * P], wq[:, :, j * P:(j + 1) * P], xnTA)
                ins.then_inc(front.sem, 1)

            def a_qp(t, c, g):
                n = 2 * c + g
                pe.wait_ge(front.sem, front.at(t, f"qk{n - 1}" if n else "qT"))
                for j in range(4):
                    for half in range(2):
                        rows = slice(DH * half, DH * half + DH)
                        ins = mm(psS[half][:, j * P:(j + 1) * P], wkT[rows, 4 * g + j, c * P:(c + 1) * P],
                                 qT[rows, 4 * g + j, :], True, True)
                ins.then_inc(front.sem, 1)

            def a_s(t, u):
                b, quarter = divmod(u, 4)
                if u == 0:
                    pe.wait_ge(front.sem, front.at(t, "qk3"))
                    pe.wait_ge(in_cx[t.par], t.landed(3))
                if u >= 2:
                    pe.wait_ge(exp_done.sem, exp_done.at(t, u - 2))
                for k in range(2):
                    j = 2 * quarter + k
                    for c in range(DC):
                        ins = mm(psS[u % 2][:, k * CTX:(k + 1) * CTX], qk[:, c, b, 2 * j:2 * j + 2, :],
                                 cxT[:, t.par, c, b, :], c == 0, c == DC - 1)
                ins.then_inc(scores_ps.sem, 1)

            def a_tr(t, u):
                pe.wait_ge(probs.sem, probs.at(t, u))
                if u:
                    pe.wait_ge(mixed.sem, mixed.at(t, u - 1))
                for kc in range(KC):
                    for k in range(2):
                        ins = pe.transpose(psW[:, (2 * kc + k) * P:(2 * kc + k + 1) * P],
                                           prA[:, u % 2, k, kc * P:(kc + 1) * P], ident[:])
                ins.then_inc(probsT_ps.sem, 1)

            def a_z(t, u):
                b = u // 4
                pe.wait_ge(probsT.sem, probsT.at(t, u))
                for c in range(DC):
                    for kc in range(KC):
                        ins = mm(psW[:, c * 2 * P:(c + 1) * 2 * P], cx[:, t.par, b * KC + kc, c * P:(c + 1) * P],
                                 prTA[:, u % 2, kc, :], kc == 0, kc == KC - 1)
                ins.then_inc(mixed_ps.sem, 1)

            def a_v(t):
                pe.wait_ge(mixed.sem, mixed.at(t, UNITS - 1))
                for h in range(H):
                    rows = slice(DH * (h % 2), DH * (h % 2) + DH)
                    j = h // 2
                    for c in range(DC):
                        ins = mm(psS[j // 4][rows, (j % 4) * P:(j % 4 + 1) * P], wv[:, c, h * DH:(h + 1) * DH],
                                 qk[:, c, :, h, :], c == 0, c == DC - 1)
                ins.then_inc(tail.sem, 1)

            def a_y(t):
                pe.wait_ge(tail.sem, tail.at(t, "oT"))
                for j in range(PAIRS):
                    ins = mm(psW[:, 0:D], oT[:, j, :], wo[:, j, :], j == 0, j == PAIRS - 1)
                ins.then_inc(tail.sem, 1)

            def scores_small(ps, q, k):
                for c in range(DC):
                    for s in range(2):
                        for b in range(2):
                            for g in range(2):
                                rows = slice(S * g, S * g + S)
                                at = ((c * 2 + s) * 2 + b) * S
                                ins = mm(ps[:, g, at:at + S], q[rows, c, b, 2 * s:2 * s + 2, :],
                                         k[rows, c, b * S:(b + 1) * S], True, True)
                return ins

            def probs_turn(ps, pr):
                for g in range(2):
                    for cs in range(4):
                        ins = pe.transpose(ps[:, g, cs * P:(cs + 1) * P], pr[:, g, cs, :], ident[:])
                return ins

            def values_small(ps, prT, v):
                for c in range(DC):
                    for g in range(2):
                        for s in range(2):
                            j = 4 * c + 2 * g + s
                            for b in range(2):
                                rows = slice(S * b, S * b + S)
                                ins = mm(ps[:, b, j * 2 * HD:(j + 1) * 2 * HD], prT[rows, g, 2 * c + s, :],
                                         v[rows, j * 2 * HD:(j + 1) * 2 * HD], True, True)
                return ins

            def b_xt(t):
                pe.wait_ge(rope.sem, rope.at(t, "xn"))
                if t.back(1).exists:
                    pe.wait_ge(ffn.sem, ffn.at(t.back(1), "added"))
                turn(psB[:, 0, 0:D], xnB[:]).then_inc(rope.sem, 1)

            def b_qkv(t):
                pe.wait_ge(rope.sem, rope.at(t, "xnT"))
                project(psB[:, 0, :], xnTB, wqkv_b[:, :, 0:2 * D])
                project(psB[:, 1, 0:D], xnTB, wqkv_b[:, :, 2 * D:3 * D]).then_inc(rope.sem, 1)

            def b_qkt(t):
                pe.wait_ge(rope.sem, rope.at(t, "roped"))
                turn(psB[:, 0, 0:D], qkB[:, 0:D])
                turn(psB[:, 1, 0:D], qkB[:, D:2 * D]).then_inc(rope.sem, 1)

            def b_s(t):
                pe.wait_ge(rope.sem, rope.at(t, "qkT"))
                scores_small(psB, qBB, kTB).then_inc(rope.sem, 1)

            def b_tr(t):
                pe.wait_ge(rope.sem, rope.at(t, "exp"))
                probs_turn(psB, prB).then_inc(rope.sem, 1)

            def b_av(t):
                pe.wait_ge(rope.sem, rope.at(t, "pT"))
                values_small(psB, prTB, vB).then_inc(rope.sem, 1)

            def b_aot(t):
                pe.wait_ge(rope.sem, rope.at(t, "heads"))
                turn(psB[:, 0, 0:D], aoB[:]).then_inc(rope.sem, 1)

            def b_wo(t):
                pe.wait_ge(rope.sem, rope.at(t, "headsT"))
                project(psB[:, 1, 0:D], aoTB, wo_b).then_inc(rope.sem, 1)

            def f_xt(t):
                pe.wait_ge(ffn.sem, ffn.at(t, "in_quant"))
                out = psB[:, 0, :].bitcast(BF16)
                for c in range(DC):
                    ins = pe.transpose(out[:, c * P:(c + 1) * P], hq[:, c * P:(c + 1) * P], identb[:])
                ins.then_inc(ffn.sem, 1)

            def f_up(t):
                pe.wait_ge(ffn.sem, ffn.at(t, "inT"))
                for n in range(2):
                    for c in range(DC):
                        ins = mm(psB[:, n, :], hqT[:, c, :], up_w[:, c, n * 512:(n + 1) * 512], c == 0, c == DC - 1)
                ins.then_inc(ffn.sem, 1)

            def f_ht(t):
                pe.wait_ge(ffn.sem, ffn.at(t, "mid_quant"))
                out = psB[:, 0, :].bitcast(BF16)
                for c in range(FF // P):
                    ins = pe.transpose(out[:, c * P:(c + 1) * P], hq[:, c * P:(c + 1) * P], identb[:])
                ins.then_inc(ffn.sem, 1)

            def f_down(t):
                pe.wait_ge(ffn.sem, ffn.at(t, "midT"))
                for c in range(FF // P):
                    ins = mm(psB[:, 1, 0:D], hqT[:, c, :], down_w[:, c, :], c == 0, c == FF // P - 1)
                ins.then_inc(ffn.sem, 1)

            def d_xt(t):
                pe.wait_ge(masked.sem, masked.at(t, "xn"))
                if t.back(1).exists:
                    pe.wait_ge(masked_out.sem, masked_out.at(t.back(1), "biased"))
                turn(psD[:, 0:D], xnD[:]).then_inc(masked.sem, 1)

            def d_g(t):
                pe.wait_ge(masked.sem, masked.at(t, "xnT"))
                for c in range(DC):
                    ins = mm(psD[:, c * P:(c + 1) * P], gx[:], xnTD[:, c, :], True, True)
                ins.then_inc(masked.sem, 1)

            def d_s(t, u):
                b, c, g = unit(u)
                if u == 0:
                    pe.wait_ge(masked.sem, masked.at(t, "q"))
                    pe.wait_ge(in_cxD, t.count(48, 48))
                if u == 1:
                    pe.wait_ge(m_masked.sem, m_masked.at(t, 0))
                if u >= 2:
                    pe.wait_ge(m_heads.sem, m_heads.at(t, u - 2))
                rows = slice(S * g, S * g + S)
                for s in range(2):
                    ins = mm(psD[:, s * CTX:(s + 1) * CTX], qBD[rows, c, b, 2 * s:2 * s + 2, :], cxTD[rows, c, b, :],
                             True, True)
                ins.then_inc(m_scores_ps.sem, 1)

            def d_tr(t, u):
                pe.wait_ge(m_exp.sem, m_exp.at(t, u))
                if u + 1 < UNITS:
                    pe.wait_ge(m_masked.sem, m_masked.at(t, u + 1))
                else:
                    pe.wait_ge(m_heads.sem, m_heads.at(t, u - 1))
                for s in range(2):
                    for kc in range(KC):
                        ins = pe.transpose(psD[:, (2 * s + kc) * P:(2 * s + kc + 1) * P],
                                           prD[:, u % 2, s, kc * P:(kc + 1) * P], ident[:])
                ins.then_inc(m_probsT_ps.sem, 1)

            def d_av(t, u):
                b, c, g = unit(u)
                pe.wait_ge(m_probsT.sem, m_probsT.at(t, u))
                for s in range(2):
                    j = 4 * c + 2 * g + s
                    for kc in range(KC):
                        ins = mm(psD[:, s * 2 * HD:(s + 1) * 2 * HD], prTD[:, s, kc, :],
                                 cxD[:, b * KC + kc, j * 2 * HD:(j + 1) * 2 * HD], kc == 0, kc == KC - 1)
                ins.then_inc(m_out_ps.sem, 1)

            def d_zt(t):
                pe.wait_ge(m_heads.sem, m_heads.at(t, UNITS - 1))
                turn(psD[:, 0:D], aoD[:]).then_inc(masked_out.sem, 1)

            def d_o(t):
                pe.wait_ge(masked_out.sem, masked_out.at(t, "headsT"))
                project(psD[:, 0:D], aoTD, vo).then_inc(masked_out.sem, 1)

            def c_xt(t):
                pe.wait_ge(alib.sem, alib.at(t, "xn"))
                if t.back(1).exists:
                    pe.wait_ge(route.sem, route.at(t.back(1), "put"))
                turn(psC[:, 0, 0:D], xnC[:]).then_inc(alib.sem, 1)

            def c_qkv(t):
                pe.wait_ge(alib.sem, alib.at(t, "xnT"))
                for c in range(DC):
                    project(psC[:, 0, c * P:(c + 1) * P], w_c[:, :, c * P:(c + 1) * P], xnTC)
                project(psC[:, 0, D:2 * D], xnTC, w_c[:, :, 2 * D:3 * D])
                for c in range(DC):
                    ins = project(psC[:, 1, c * P:(c + 1) * P], w_c[:, :, D + c * P:D + (c + 1) * P], xnTC)
                ins.then_inc(alib.sem, 1)

            def c_s(t):
                pe.wait_ge(alib.sem, alib.at(t, "qkv"))
                scores_small(psC, qBC, kTC).then_inc(alib.sem, 1)

            def c_tr(t):
                pe.wait_ge(alib.sem, alib.at(t, "exp"))
                probs_turn(psC, prC).then_inc(alib.sem, 1)

            def c_av(t):
                pe.wait_ge(alib.sem, alib.at(t, "pT"))
                values_small(psC, prTC, vC).then_inc(alib.sem, 1)

            def c_aot(t):
                pe.wait_ge(alib.sem, alib.at(t, "heads"))
                turn(psC[:, 0, 0:D], aoC[:]).then_inc(alib.sem, 1)

            def c_wo(t):
                pe.wait_ge(alib.sem, alib.at(t, "headsT"))
                project(psC[:, 1, 0:D], aoTC, wo_c).then_inc(alib.sem, 1)

            def m_xt(t):
                pe.wait_ge(route.sem, route.at(t, "xn"))
                turn(psC[:, 0, 0:D], xnM[:, t.par, :]).then_inc(route.sem, 1)

            def m_gu(t):
                pe.wait_ge(route.sem, route.at(t, "xnT"))
                for n in range(2):
                    project(psC[:, 0, n * P:(n + 1) * P], sw13[:, :, n * P:(n + 1) * P], xnTC)
                project(psC[:, 1, 0:E], xnTC, gate_w).then_inc(route.sem, 1)

            def m_out(t):
                pe.wait_ge(route.sem, route.at(t, "gates"))
                mm(psC[:, 1, 0:E], beforeb[:], sel[:], True, False)
                mm(psC[:, 1, 0:E], onesb[:], seen[:], False, True)
                mm(psC[:, 0, 0:D], shared[:, 1, :], sw2[:], True, True).then_inc(route.sem, 1)

            run(pe, {k: v for k, v in locals().items() if k in STAGE_NAMES})

            def expert_turn(e):
                p = e.par
                pe.wait_ge(ex_in[p], e.landed(4))
                for c in range(DC):
                    for k in range(KC):
                        ins = pe.transpose(psB[:, p, (2 * c + k) * P:(2 * c + k + 1) * P],
                                           ex_x[:, p, k, c * P:(c + 1) * P], ident[:])
                ins.then_inc(ex_xT_ps.sem, 1)

            def expert_up(e):
                p = e.par
                pe.wait_ge(ex_xT_in.sem, ex_xT_in.at(e, 0))
                pe.wait_ge(ex_weights.sem, ex_weights.at(e, 0))
                for n in range(2):
                    for c in range(DC):
                        ins = mm(psS[p][:, n * CAP:(n + 1) * CAP], ex_w13f[:, c, n * EI:(n + 1) * EI],
                                 ex_xT[:, p, c, :], c == 0, c == DC - 1)
                ins.then_inc(ex_up_ps.sem, 1)

            def expert_down(e):
                p = e.par
                pe.wait_ge(ex_act.sem, ex_act.at(e, "h"))
                for k in range(KC):
                    ins = mm(psC[:, p, k * D:(k + 1) * D], ex_h[:, p, 1, k * P:(k + 1) * P], ex_w2f[:, p, :], True, True)
                ins.then_inc(ex_down_ps.sem, 1)

            skewed(pe, (expert_turn, 0), (expert_up, 1), (expert_down, 2))

        @block.scalar
        def _(act):
            copy = lambda out, in_: act.activation(out, in_, ACT.Copy)
            act.wait_ge(s_once, 16 * len(once))
            copy(gate_w[:], gate_bf).then_inc(s_setup_act, 1)
            copy(sw13[:], sw13_bf).then_inc(s_setup_act, 1)
            copy(sw2[:], sw2_bf).then_inc(s_setup_act, 1)
            act.wait_ge(s_setup_pool, 4)
            zero_rows = expert_in.rearrange("(n p r) d -> n p (r d)", p=P, r=4)
            for n in range(E * CAP // (4 * P)):
                act.dma_start(zero_rows[n], hid[:]).then_inc(s_zero, 16)

            def a_xt(t):
                act.wait_ge(front.sem, front.at(t, "xnT_ps"))
                copy(xnTA[:].rearrange("p c n -> p (c n)"), psW[:, 0:D]).then_inc(front.sem, 1)

            def a_q(t):
                act.wait_ge(front.sem, front.at(t, "qT_ps"))
                act.activation(qT[:, 0:4, :].rearrange("p j n -> p (j n)"), psS[0][:], ACT.Copy,
                               scale=DH ** -0.5).then_inc(front.sem, 1)

            def a_qp(t, c, g):
                act.wait_ge(front.sem, front.at(t, f"qk_ps{2 * c + g}"))
                copy(qk[:, c, :, 8 * g:8 * g + 8:2, :].rearrange("p b h s -> p h b s"),
                     psS[0][:].rearrange("p (h b s) -> p h b s", h=4, b=2)).then_inc(front.sem, 1)

            def a_s(t, u):
                act.wait_ge(neg_max.sem, neg_max.at(t, u))
                for k in range(2):
                    ins = act.activation(prA[:, u % 2, k, :], psS[u % 2][:, k * CTX:(k + 1) * CTX], ACT.Exp,
                                         bias=smA[:, u % 2, 0, k:k + 1], accum_out=smA[:, u % 2, 1, k:k + 1])
                ins.then_inc(exp_done.sem, 1)

            def a_n(t, u):
                act.wait_ge(inv_sum.sem, inv_sum.at(t, u))
                for k in range(2):
                    ins = act.activation(prA[:, u % 2, k, :], prA[:, u % 2, k, :], ACT.Copy, scale=smA[:, u % 2, 2, k:k + 1])
                ins.then_inc(probs.sem, 1)

            def a_tr(t, u):
                act.wait_ge(probsT_ps.sem, probsT_ps.at(t, u))
                if u >= 2:
                    act.wait_ge(mixed_ps.sem, mixed_ps.at(t, u - 2))
                copy(prTA[:, u % 2].rearrange("p k n -> p (k n)"), psW[:]).then_inc(probsT.sem, 1)

            def a_z(t, u):
                b, quarter = divmod(u, 4)
                act.wait_ge(mixed_ps.sem, mixed_ps.at(t, u))
                copy(qk[:, :, b, 4 * quarter:4 * quarter + 4, :],
                     psW[:].rearrange("p (c h s) -> p c h s", c=DC, h=4)).then_inc(mixed.sem, 1)

            def a_v(t):
                act.wait_ge(tail.sem, tail.at(t, "v_ps"))
                copy(oT[:, 0:4, :].rearrange("p j n -> p (j n)"), psS[0][:]).then_inc(tail.sem, 1)

            def flat(x):
                return x[:].rearrange("p c n -> p (c n)")

            def b_xt(t):
                act.wait_ge(rope.sem, rope.at(t, "xnT_ps"))
                copy(flat(xnTB), psB[:, 0, 0:D]).then_inc(rope.sem, 1)

            def b_qkt(t):
                act.wait_ge(rope.sem, rope.at(t, "qkT_ps"))
                copy(flat(kTB), psB[:, 1, 0:D]).then_inc(rope.sem, 1)

            def b_s(t):
                act.wait_ge(rope.sem, rope.at(t, "shifted"))
                act.activation(prB[:], prB[:], ACT.Exp, scale=HD ** -0.5).then_inc(rope.sem, 1)

            def b_tr(t):
                act.wait_ge(rope.sem, rope.at(t, "pT_ps"))
                copy(prTB[:, 0].rearrange("p c n -> p (c n)"), psB[:, 0, :]).then_inc(rope.sem, 1)

            def b_aot(t):
                act.wait_ge(rope.sem, rope.at(t, "headsT_ps"))
                copy(flat(aoTB), psB[:, 0, 0:D]).then_inc(rope.sem, 1)

            def squares(t, src, before_, dst):
                act.wait_ge(ffn.sem, ffn.at(t, before_))
                act.activation(sq[:, 0:src.shape[-1]], src, ACT.Square, accum_out=dst).then_inc(ffn.sem, 1)

            def f_nx(t):
                squares(t, xnB[:], "xn", stB[:, 16:17])

            def f_q2(t):
                act.wait_ge(ffn.sem, ffn.at(t, "in_rounded"))
                act.activation(hq[:, 0:D], hid[:, 0:D], ACT.Copy, bias=-MAGIC).then_inc(ffn.sem, 1)

            def f_xt(t):
                act.wait_ge(ffn.sem, ffn.at(t, "inT_ps"))
                copy(hqT[:, 0:DC, :].rearrange("p c n -> p (c n)"), psB[:, 0, :].bitcast(BF16)[:, 0:D]).then_inc(ffn.sem, 1)

            def f_up(t):
                act.wait_ge(ffn.sem, ffn.at(t, "up_ps"))
                for n in range(2):
                    act.activation(hid[:, n * 512:(n + 1) * 512], psB[:, n, :], ACT.Relu,
                                   scale=stB[:, 22:23]).then_inc(ffn.sem, 1)
                act.wait_ge(ffn.sem, ffn.at(t, "relu"))
                act.activation(hid[:], hid[:], ACT.Square).then_inc(ffn.sem, 1)
                act.wait_ge(ffn.sem, ffn.at(t, "square"))
                act.activation(hid[:], hid[:], ACT.Identity, scale=act_sc[:, 0:1], bias=act_bi[:, 0:1]).then_inc(ffn.sem, 1)

            def f_w(t):
                squares(t, hid[:], "affine", stB[:, 16:17])

            def f_q5(t):
                act.wait_ge(ffn.sem, ffn.at(t, "mid_rounded"))
                act.activation(hq[:], g2, ACT.Copy, bias=-MAGIC).then_inc(ffn.sem, 1)

            def f_ht(t):
                act.wait_ge(ffn.sem, ffn.at(t, "midT_ps"))
                copy(hqT[:].rearrange("p c n -> p (c n)"), psB[:, 0, :].bitcast(BF16)).then_inc(ffn.sem, 1)

            def d_xt(t):
                act.wait_ge(masked.sem, masked.at(t, "xnT_ps"))
                copy(flat(xnTD), psD[:, 0:D]).then_inc(masked.sem, 1)

            def d_s(t, u):
                act.wait_ge(m_masked.sem, m_masked.at(t, u))
                for s in range(2):
                    pr = prD[:, u % 2, s, :]
                    ins = act.activation(pr, pr, ACT.Exp, scale=-1.0, bias=smD[:, u % 2, 0, s:s + 1],
                                         accum_out=smD[:, u % 2, 1, s:s + 1])
                ins.then_inc(m_exp.sem, 1)

            def d_tr(t, u):
                act.wait_ge(m_probsT_ps.sem, m_probsT_ps.at(t, u))
                copy(prTD[:].rearrange("p s k n -> p (s k n)"), psD[:]).then_inc(m_probsT.sem, 1)

            def d_zt(t):
                act.wait_ge(masked_out.sem, masked_out.at(t, "headsT_ps"))
                copy(flat(aoTD), psD[:, 0:D]).then_inc(masked_out.sem, 1)

            def c_xt(t):
                act.wait_ge(alib.sem, alib.at(t, "xnT_ps"))
                copy(flat(xnTC), psC[:, 0, 0:D]).then_inc(alib.sem, 1)

            def c_qkv(t):
                act.wait_ge(alib.sem, alib.at(t, "qkv_ps"))
                for c in range(DC):
                    act.activation(kTC[:, c, :], psC[:, 1, c * P:(c + 1) * P], ACT.Identity,
                                   bias=bqk_c[:, 1, c:c + 1]).then_inc(alib.sem, 1)

            def c_s(t):
                act.wait_ge(alib.sem, alib.at(t, "shifted"))
                act.activation(prC[:], prC[:], ACT.Exp).then_inc(alib.sem, 1)

            def c_tr(t):
                act.wait_ge(alib.sem, alib.at(t, "pT_ps"))
                copy(prTC[:, 0].rearrange("p c n -> p (c n)"), psC[:, 0, :]).then_inc(alib.sem, 1)

            def c_aot(t):
                act.wait_ge(alib.sem, alib.at(t, "headsT_ps"))
                copy(flat(aoTC), psC[:, 0, 0:D]).then_inc(alib.sem, 1)

            def m_xt(t):
                act.wait_ge(route.sem, route.at(t, "xnT_ps"))
                copy(flat(xnTC), psC[:, 0, 0:D]).then_inc(route.sem, 1)

            def m_gu(t):
                act.wait_ge(route.sem, route.at(t, "up_ps"))
                act.activation(shared[:, 0, :], psC[:, 0, 0:P], ACT.Exp, scale=-1.0).then_inc(route.sem, 1)
                act.activation(gl[:, 0, :], psC[:, 1, 0:E], ACT.Exp, scale=-1.0).then_inc(route.sem, 1)

            run(act, {k: v for k, v in locals().items() if k in STAGE_NAMES})

            def expert_turn(e):
                p = e.par
                act.wait_ge(ex_xT_ps.sem, ex_xT_ps.at(e, 0))
                copy(flat(ex_xT[:, p]), psB[:, p, :]).then_inc(ex_xT_in.sem, 1)

            def expert_up(e):
                p = e.par
                act.wait_ge(ex_up_ps.sem, ex_up_ps.at(e, 0))
                act.activation(ex_h[:, p, 0, :], psS[p][:, 0:CAP], ACT.Exp, scale=-1.0).then_inc(ex_exp.sem, 1)

            def expert_down(e):
                p = e.par
                act.wait_ge(ex_meta_in[p], e.loads())
                act.wait_ge(ex_down_ps.sem, ex_down_ps.at(e, 0))
                if e.back(2).exists:
                    act.wait_ge(ex_added, added(e.back(2)))
                for k in range(KC):
                    ins = act.activation(ex_y[:, p, k, :], psC[:, p, k * D:(k + 1) * D], ACT.Copy,
                                         scale=ex_meta[:, p, k, 1:2].bitcast(F32))
                ins.then_inc(ex_rows.sem, 1)

            skewed(act, (expert_turn, 0), (expert_up, 1), (expert_down, 2))

        @block.gpsimd
        def _(pool):
            below_last, bound = pool.to_reg(E * CAP - 2), pool.alloc_register("bound")
            below_spare = pool.to_reg(TILES * P + CAP - 2)
            pool.memset(diag, 0.0).then_inc(s_setup_pool, 1)
            pool.memset(seen[:], 0.0).then_inc(s_setup_pool, 1)
            pool.memset(neg_half[:], -0.5).then_inc(s_setup_pool, 1)
            pool.memset(hid[:], 0.0).then_inc(s_setup_pool, 1)
            pool.memset(ones[:], 1.0).then_inc(s_setup_pool, 1)
            pool.memset(onesb[:], 1.0).then_inc(s_setup_pool, 1)
            pool.memset(stC[:], 0.0).then_inc(s_setup_pool, 1)

            def rstd(chain, st, src="var", at=8):
                def stage(t):
                    pool.wait_ge(chain.sem, chain.at(t, src))
                    pool.tensor_tensor(st[:, at + 1:at + 2], st[:, at:at + 1], neg_half[:], ALU.pow).then_inc(chain.sem, 1)
                return stage

            a_ln, b_ln, d_ln = rstd(front, stA), rstd(rope, stB), rstd(masked, stD)
            c_ln, m_ln = rstd(alib, stC), rstd(route, stC)

            f_ln = rstd(ffn, stB)
            f_q1, f_q3 = rstd(ffn, stB, "in_var", 17), rstd(ffn, stB, "mid_var", 17)

            def b_qkv(t):
                pool.wait_ge(rope.sem, rope.at(t, "qkv"))
                q = qkB[:].rearrange("p (h two e) -> p h two e", two=2, e=HD // 2)
                r = rot.rearrange("p (h two e) -> p h two e", two=2, e=HD // 2)
                sin = rope_sin[:].rearrange("p (h two e) -> p h two e", two=2, e=HD // 2)
                for n in range(2):
                    pool.tensor_tensor(r[:, :, n, :], q[:, :, 1 - n, :], sin[:, :, n, :], ALU.mult).then_inc(rope.sem, 1)

            def d_xt(t):
                pool.wait_ge(in_mask, t.count(32, 32))
                if t.back(1).exists:
                    pool.wait_ge(masked_out.sem, masked_out.at(t.back(1), "biased"))
                pool.tensor_tensor(carrier[:, 0:1], neg_half[:], neg_half[:], ALU.add)
                pool.tensor_scalar(mask_add[:], mask[:], 0.0, 1e20 * D ** -0.5, ALU.is_equal, ALU.mult
                                   ).then_inc(mask_ready.sem, 1)

            def m_put(t):
                if t.i is None and t.c == 0:
                    pool.wait_ge(s_zero, 16 * (E * CAP // (4 * P)))
                    pool.wait_ge(s_tables, 32)
                pool.wait_ge(route.sem, route.at(t, "put"))
                pool.reg_add(bound, below_last, 1)
                for k in range(TOPK):
                    for table, src in ((expert_in, xnM[:, t.par, :]), (places, row_meta[:, t.par, k, :])):
                        pool.indirect_dma_start(
                            out=table, out_offset=bass.IndirectOffsetOnAxis(ap=put[:, t.par, k:k + 1].bitcast(U32), axis=0),
                            in_=src, in_offset=None, bounds_check=bound, oob_is_err=False,
                        ).then_inc(scattered[t.par], 16)

            run(pool, {k: v for k, v in locals().items() if k in STAGE_NAMES})

            for p in range(2):
                pool.wait_ge(out_part[p], 16 * (TILES // 2))

            for p in range(2):
                pool.wait_ge(scattered[p], 16 * 2 * TOPK * (TILES // 2))

            def load_meta(e):
                pool.dma_start(ex_meta[:, e.par], places[bass.ts(e.row(), CAP), :].rearrange("(k p) t -> p k t", p=P)
                               ).then_inc(ex_meta_in[e.par], 16)

            load_meta(Tile(0))

            def expert_weights(e):
                p = e.par
                pool.wait_ge(ex_in[p], e.landed(4))
                if e.back(1).exists:
                    pool.wait_ge(ex_up_ps.sem, ex_up_ps.at(e.back(1), 0))
                if e.back(2).exists:
                    pool.wait_ge(ex_down_ps.sem, ex_down_ps.at(e.back(2), 0))
                pool.tensor_tensor(carrier[:, 0:1], neg_half[:], neg_half[:], ALU.add)
                pool.tensor_copy(ex_w2f[:, p, :], ex_w2[:, p, :])
                pool.tensor_copy(ex_w13f, ex_w13[:, p]).then_inc(ex_weights.sem, 1)

            def expert_add(e):
                p = e.par
                pool.wait_ge(ex_rows.sem, ex_rows.at(e, 0))
                if e.back(1).exists:
                    pool.reg_add(bound, below_spare, 1)
                    pool.wait_ge(ex_added, added(e.back(1)))
                pool.reg_add(bound, below_spare, 1)
                if e.i is not None or e.c + 1 < E:
                    load_meta(e.back(-1))
                for k in range(KC):
                    pool.indirect_dma_start(
                        out=a["out"], out_offset=bass.IndirectOffsetOnAxis(ap=ex_meta[:, p, k, 0:1].bitcast(U32), axis=0),
                        in_=ex_y[:, p, k, :], in_offset=None, compute_op=ALU.add, bounds_check=bound,
                        oob_is_err=True).then_inc(ex_added, 16)

            skewed(pool, (expert_weights, 0), (expert_add, 2))

        @block.vector
        def _(dve):
            def carry():
                dve.memset(carrier[:, 1:2], 0.0)

            def wide(x, n):
                return x.unsqueeze(2).broadcast_to([P, x.shape[1], n])

            dve.wait_ge(s_once, 16 * len(once))
            dve.tensor_reduce(wsum[:, 0:1], raw[:, 0:DC * FF], AX.X, ALU.add, apply_absolute_value=True).then_inc(s_setup_dve, 1)
            dve.tensor_reduce(wsum[:, 1:2], raw[:, DC * FF:2 * DC * FF], AX.X, ALU.add, apply_absolute_value=True).then_inc(s_setup_dve, 1)
            dve.wait_ge(s_setup_pe, 2)
            dve.tensor_scalar(wmean[:], psW[:, 0:2], 1.0 / (D * FF), EPS, ALU.mult, ALU.max).then_inc(s_setup_dve, 1)
            dve.wait_ge(s_setup_dve, 3)
            dve.reciprocal(wscale[:], wmean[:]).then_inc(s_setup_dve, 1)
            dve.tensor_scalar(wdeq[:], wmean[:], 1.0 / 127.0, None, ALU.mult).then_inc(s_setup_dve, 1)
            n = 5
            for k, out in enumerate((up_w, down_w)):
                w = raw[:, k * DC * FF:(k + 1) * DC * FF]
                dve.wait_ge(s_setup_dve, n)
                dve.tensor_scalar(w, w, wscale[:, k:k + 1], -1.0, ALU.mult, ALU.max).then_inc(s_setup_dve, 1)
                dve.wait_ge(s_setup_dve, n + 1)
                dve.tensor_scalar(w, w, 1.0, MAGIC, ALU.min, ALU.add).then_inc(s_setup_dve, 1)
                dve.wait_ge(s_setup_dve, n + 2)
                dve.tensor_scalar(out[:].rearrange("p c n -> p (c n)"), w, -MAGIC, None, ALU.add).then_inc(s_setup_dve, 1)
                n += 3
            dve.tensor_scalar(gx[:], psW[:, P:2 * P], -(D ** -0.5), None, ALU.mult)
            dve.tensor_copy(vo[:].rearrange("p c n -> p (c n)"), psS[0][:])
            dve.tensor_copy(identb[:], ident[:])
            dve.tensor_copy(beforeb[:], before).then_inc(s_setup_dve, 3)

            def norm(chain, st, src, out, source_ready):
                def statistics(t):
                    source_ready(t)
                    dve.bn_stats(st[:, 0:6], src(t)).then_inc(chain.sem, 1)
                    dve.wait_ge(chain.sem, chain.at(t, "stats"))
                    carry()
                    dve.bn_aggr(st[:, 6:8], st[:, 0:6]).then_inc(chain.sem, 1)
                    dve.wait_ge(chain.sem, chain.at(t, "mean"))
                    dve.tensor_scalar(st[:, 8:9], st[:, 7:8], EPS, None, ALU.add).then_inc(chain.sem, 1)

                def normalised(t):
                    dve.wait_ge(chain.sem, chain.at(t, "rstd"))
                    dve.tensor_scalar(out(t), src(t), st[:, 6:7], st[:, 9:10], ALU.subtract, ALU.mult).then_inc(chain.sem, 1)
                return statistics, normalised

            def a_ready(t):
                dve.wait_ge(in_x[t.par], t.loads())

            a_ln, a_nx = norm(front, stA, lambda t: xa[:, t.par, :], lambda t: xnA[:], a_ready)

            def a_q(t):
                dve.wait_ge(front.sem, front.at(t, "qT_ps"))
                dve.tensor_scalar(qT[:, 4:8, :].rearrange("p j n -> p (j n)"), psS[1][:], DH ** -0.5, None, ALU.mult
                                  ).then_inc(front.sem, 1)

            def a_qp(t, c, g):
                dve.wait_ge(front.sem, front.at(t, f"qk_ps{2 * c + g}"))
                dve.tensor_copy(qk[:, c, :, 8 * g + 1:8 * g + 8:2, :].rearrange("p b h s -> p h b s"),
                                psS[1][:].rearrange("p (h b s) -> p h b s", h=4, b=2)).then_inc(front.sem, 1)

            def a_s(t, u):
                dve.wait_ge(scores_ps.sem, scores_ps.at(t, u))
                dve.tensor_reduce(smA[:, u % 2, 0, :], psS[u % 2][:].rearrange("p (k n) -> p k n", k=2), AX.X, ALU.max,
                                  negate=True).then_inc(neg_max.sem, 1)

            def a_n(t, u):
                dve.wait_ge(exp_done.sem, exp_done.at(t, u))
                dve.reciprocal(smA[:, u % 2, 2, :], smA[:, u % 2, 1, :]).then_inc(inv_sum.sem, 1)

            def a_v(t):
                dve.wait_ge(tail.sem, tail.at(t, "v_ps"))
                dve.tensor_copy(oT[:, 4:8, :].rearrange("p j n -> p (j n)"), psS[1][:]).then_inc(tail.sem, 1)

            def a_y(t):
                dve.wait_ge(tail.sem, tail.at(t, "y_ps"))
                if t.back(2).exists:
                    dve.wait_ge(ffn.sem, ffn.at(t.back(2), "added"))
                dve.tensor_tensor(xb[:, t.par, :], psW[:, 0:D], xa[:, t.par, :], ALU.add).then_inc(tail.sem, 1)

            def masked_heads(chain, t, wait_for, ps, out):
                dve.wait_ge(chain.sem, chain.at(t, wait_for))
                for m in range(4):
                    dve.tensor_scalar(out[:, :, :, m, :], ps.rearrange("p (c b s) -> p c b s", c=DC, b=2),
                                      head_mask[:, m:m + 1], None, ALU.mult).then_inc(chain.sem, 1)

            def shift_small(chain, t, scores, pr, sm):
                sc = scores.rearrange("p g (n k) -> p (g n) k", k=S)
                prv = pr[:].rearrange("p g c (b k) -> p (g c b) k", k=S)
                dve.tensor_reduce(sm[:, 0, :], sc, AX.X, ALU.max).then_inc(chain.sem, 1)
                dve.wait_ge(chain.sem, chain.at(t, "max"))
                dve.tensor_tensor(prv, sc, wide(sm[:, 0, :], S), ALU.subtract).then_inc(chain.sem, 1)

            def sums_small(chain, sums, t, pr, sm):
                dve.wait_ge(chain.sem, chain.at(t, "exp"))
                for g in range(2):
                    dve.tensor_reduce(sm[:, 1, :].rearrange("p (c g n) -> p c g n", c=DC, g=2)[:, :, g, :],
                                      pr[:, g].rearrange("p (c s) (b k) -> p c (s b) k", c=DC, k=S), AX.X, ALU.add
                                      ).then_inc(sums.sem, 1)
                dve.wait_ge(sums.sem, sums.at(t, "sum"))
                dve.reciprocal(sm[:, 2, :], sm[:, 1, :]).then_inc(sums.sem, 1)

            def second_half_turned(chain, t, ps_step, ps, prT):
                dve.wait_ge(chain.sem, chain.at(t, ps_step))
                dve.tensor_copy(prT[:, 1].rearrange("p c n -> p (c n)"), ps[:, 1, :]).then_inc(chain.sem, 1)

            def heads_small(chain, sums, t, ps, sm, out):
                dve.wait_ge(sums.sem, sums.at(t, "inverse"))
                dve.wait_ge(chain.sem, chain.at(t, "out_ps"))
                for b in range(2):
                    for half in range(2):
                        rows = slice(S * half, S * half + S)
                        inv = sm[rows, 2, b:16:2].unsqueeze(2).broadcast_to([S, PAIRS, HD])
                        dve.tensor_tensor(
                            out[S * b:S * b + S, :].rearrange("p (j two e) -> p j two e", two=2, e=HD)[:, :, half, :],
                            ps[rows, b, 0:D].rearrange("p (j two e) -> p j two e", two=2, e=HD)[:, :, half, :],
                            inv, ALU.mult).then_inc(chain.sem, 1)

            def add_out(chain, t, ps, x, bias, out):
                dve.wait_ge(chain.sem, chain.at(t, "proj_ps"))
                dve.tensor_tensor(out, ps, x, ALU.add).then_inc(chain.sem, 1)
                dve.wait_ge(chain.sem, chain.at(t, "added"))
                dve.tensor_tensor(out, out, bias[:], ALU.add).then_inc(chain.sem, 1)

            def b_ready(t):
                dve.wait_ge(tail.sem, tail.at(t, "x1"))
                if t.back(1).exists:
                    dve.wait_ge(ffn.sem, ffn.at(t.back(1), "added"))

            xb_of = lambda t: xb[:, t.par, :]
            b_ln, b_nx = norm(rope, stB, xb_of, lambda t: xnB[:], b_ready)

            def b_qkv(t):
                if t.i is None and t.c == 0:
                    dve.wait_ge(s_zero, 16 * (E * CAP // (4 * P)))
                dve.wait_ge(rope.sem, rope.at(t, "qkv_ps"))
                dve.tensor_tensor(qkB[:], psB[:, 0, :], bqkv[:, 0:2 * D], ALU.add).then_inc(rope.sem, 1)
                dve.tensor_tensor(vB[:], psB[:, 1, 0:D], bqkv[:, 2 * D:], ALU.add).then_inc(rope.sem, 1)
                dve.wait_ge(rope.sem, rope.at(t, "qkv"))
                dve.tensor_tensor(qcos, qkB[:], rope_cos[:], ALU.mult).then_inc(rope.sem, 1)

            def b_ro(t):
                dve.wait_ge(rope.sem, rope.at(t, "turned"))
                dve.tensor_tensor(qkB[:], qcos, rot, ALU.add).then_inc(rope.sem, 1)

            def b_qkt(t):
                masked_heads(rope, t, "qkT_ps", psB[:, 0, 0:D], qBB)

            def b_s(t):
                dve.wait_ge(rope.sem, rope.at(t, "scores_ps"))
                shift_small(rope, t, psB[:], prB, smB)

            def b_n(t):
                sums_small(rope, rope_sums, t, prB, smB)

            def b_tr(t):
                second_half_turned(rope, t, "pT_ps", psB, prTB)

            def b_av(t):
                heads_small(rope, rope_sums, t, psB, smB, aoB)

            def b_wo(t):
                add_out(rope, t, psB[:, 1, 0:D], xb_of(t), bo_b, xb_of(t))

            f_ln, f_normalised = norm(ffn, stB, xb_of, lambda t: xnB[:], lambda t: dve.wait_ge(rope.sem, rope.at(t, "biased")))

            col = lambda k: stB[:, k:k + 1]

            def peak(t, tag, before_, g, n):
                dve.wait_ge(ffn.sem, ffn.at(t, before_))
                dve.tensor_scalar(col(17), col(16), 1.0 / n, 1e-8, ALU.mult, ALU.add).then_inc(ffn.sem, 1)
                dve.tensor_reduce(col(19), g, AX.X, ALU.max, apply_absolute_value=True).then_inc(ffn.sem, 1)

            def quantise(t, tag, g, n, w):
                dve.wait_ge(ffn.sem, ffn.at(t, tag + "rstd"))
                dve.tensor_scalar(col(20), col(19), col(18), EPS, ALU.mult, ALU.max).then_inc(ffn.sem, 1)
                dve.wait_ge(ffn.sem, ffn.at(t, tag + "guarded"))
                dve.reciprocal(col(21), col(20)).then_inc(ffn.sem, 1)
                dve.tensor_tensor(col(22), col(20), wdeq[:, w:w + 1], ALU.mult).then_inc(ffn.sem, 1)
                dve.wait_ge(ffn.sem, ffn.at(t, tag + "inverse"))
                dve.tensor_scalar(col(23), col(21), 127.0, col(18), ALU.mult, ALU.mult).then_inc(ffn.sem, 1)
                dve.wait_ge(ffn.sem, ffn.at(t, tag + "factor"))
                dve.tensor_scalar(g, g, col(23), -128.0, ALU.mult, ALU.max).then_inc(ffn.sem, 1)

            def rounding(t, tag, g):
                dve.wait_ge(ffn.sem, ffn.at(t, tag + "clipped"))
                dve.tensor_scalar(g, g, 127.0, MAGIC, ALU.min, ALU.add).then_inc(ffn.sem, 1)

            def f_nx(t):
                f_normalised(t)
                dve.wait_ge(ffn.sem, ffn.at(t, "xn"))
                dve.tensor_tensor(hid[:, 0:D], xnB[:], norm1[:], ALU.mult).then_inc(ffn.sem, 1)

            def f_q1(t):
                peak(t, "in_", "weighed", hid[:, 0:D], D)

            def f_q2(t):
                quantise(t, "in_", hid[:, 0:D], D, 0)
                rounding(t, "in_", hid[:, 0:D])

            def f_w(t):
                dve.wait_ge(ffn.sem, ffn.at(t, "affine"))
                dve.tensor_tensor(g2, hid[:], norm2[:], ALU.mult).then_inc(ffn.sem, 1)

            def f_q3(t):
                peak(t, "mid_", "weighed2", g2, FF)

            def f_q4(t):
                quantise(t, "mid_", g2, FF, 1)

            def f_q5(t):
                rounding(t, "mid_", g2)

            def f_down(t):
                dve.wait_ge(ffn.sem, ffn.at(t, "down_ps"))
                if t.back(2).exists:
                    dve.wait_ge(masked_out.sem, masked_out.at(t.back(2), "biased"))
                dve.scalar_tensor_tensor(out=xd[:, t.par, :], in0=psB[:, 1, 0:D], scalar=stB[:, 22:23], in1=xb_of(t),
                                         op0=ALU.mult, op1=ALU.add).then_inc(ffn.sem, 1)

            def d_ready(t):
                dve.wait_ge(ffn.sem, ffn.at(t, "added"))
                if t.back(1).exists:
                    dve.wait_ge(masked_out.sem, masked_out.at(t.back(1), "biased"))

            d_ln, d_nx = norm(masked, stD, lambda t: xd[:, t.par, :], lambda t: xnD[:], d_ready)

            def d_g(t):
                masked_heads(masked, t, "q_ps", psD[:, 0:D], qBD)

            def d_s(t, u):
                dve.wait_ge(m_scores_ps.sem, m_scores_ps.at(t, u))
                if u == 0:
                    dve.wait_ge(mask_ready.sem, mask_ready.at(t, 0))
                carry()
                for s in range(2):
                    ins = dve.tensor_tensor_reduce(prD[:, u % 2, s, :], psD[:, s * CTX:(s + 1) * CTX],
                                                   mask_add[:, u // 4, :], 1.0, 3.0e38, ALU.add, ALU.min,
                                                   smD[:, u % 2, 0, s:s + 1])
                ins.then_inc(m_masked.sem, 1)

            def d_tr(t, u):
                dve.wait_ge(m_exp.sem, m_exp.at(t, u))
                dve.reciprocal(smD[:, u % 2, 2, :], smD[:, u % 2, 1, :]).then_inc(m_inverse.sem, 1)

            def d_av(t, u):
                b, c, g = unit(u)
                dve.wait_ge(m_inverse.sem, m_inverse.at(t, u))
                dve.wait_ge(m_out_ps.sem, m_out_ps.at(t, u))
                for half in range(2):
                    rows = slice(S * half, S * half + S)
                    first = (4 * c + 2 * g) * 2 * HD
                    ins = dve.tensor_tensor(
                        aoD[S * b:S * b + S, first:first + 4 * HD].rearrange("p (s two e) -> p s two e", two=2, e=HD)[:, :, half, :],
                        psD[rows, 0:4 * HD].rearrange("p (s two e) -> p s two e", two=2, e=HD)[:, :, half, :],
                        smD[rows, u % 2, 2, :].unsqueeze(2).broadcast_to([S, 2, HD]), ALU.mult)
                ins.then_inc(m_heads.sem, 1)

            def d_o(t):
                if t.back(2).exists:
                    if t.back(2).exists:
                        dve.wait_ge(route.sem, route.at(t.back(2), "put"))
                add_out(masked_out, t, psD[:, 0:D], xd[:, t.par, :], bo_x, xc[:, t.par, :])

            def c_ready(t):
                dve.wait_ge(masked_out.sem, masked_out.at(t, "biased"))
                if t.back(1).exists:
                    dve.wait_ge(route.sem, route.at(t.back(1), "put"))

            xc_of = lambda t: xc[:, t.par, :]
            c_ln, c_nx = norm(alib, stC, xc_of, lambda t: xnC[:], c_ready)

            def c_qkv(t):
                dve.wait_ge(alib.sem, alib.at(t, "qkv_ps"))
                for c in range(DC):
                    for m in range(4):
                        dve.tensor_scalar(qBC[:, c, :, m, :], psC[:, 0, c * P:(c + 1) * P].rearrange("p (b s) -> p b s", b=2),
                                          bqk_c[:, 0, c:c + 1], head_mask[:, m:m + 1], ALU.add, ALU.mult
                                          ).then_inc(alib.sem, 1)
                dve.tensor_tensor(vC[:], psC[:, 0, D:2 * D], bv_c[:], ALU.add).then_inc(alib.sem, 1)

            def c_s(t):
                dve.wait_ge(alib.sem, alib.at(t, "scores_ps"))
                for b in range(2):
                    dve.scalar_tensor_tensor(
                        out=prC[:].rearrange("p g c (b k) -> p (g c) b k", b=2)[:, :, b, :],
                        in0=psC[:].rearrange("p g (c b k) -> p (g c) b k", b=2, k=S)[:, :, b, :], scalar=HD ** -0.5,
                        in1=alibi[:].rearrange("p (j k) -> p j k", k=S), op0=ALU.mult, op1=ALU.add).then_inc(alib.sem, 1)
                dve.wait_ge(alib.sem, alib.at(t, "alibi"))
                shift_small(alib, t, prC[:].rearrange("p g c n -> p g (c n)"), prC, smC)

            def c_n(t):
                sums_small(alib, alib_sums, t, prC, smC)

            def c_tr(t):
                second_half_turned(alib, t, "pT_ps", psC, prTC)

            def c_av(t):
                heads_small(alib, alib_sums, t, psC, smC, aoC)

            def c_wo(t):
                add_out(alib, t, psC[:, 1, 0:D], xc_of(t), bo_c, xc_of(t))

            def m_ready(t):
                dve.wait_ge(alib.sem, alib.at(t, "biased"))
                if t.back(2).exists:
                    dve.wait_ge(scattered[t.par], t.back(2).landed(2 * TOPK))
                    dve.wait_ge(out_part[t.par], t.back(2).landed(1))

            m_ln, m_nx = norm(route, stC, xc_of, lambda t: xnM[:, t.par, :], m_ready)

            def m_g1(t):
                dve.wait_ge(route.sem, route.at(t, "exp"))
                dve.tensor_scalar(shared[:, 0, :], shared[:, 0, :], 1.0, None, ALU.add).then_inc(route.sem, 1)
                dve.tensor_scalar(gl[:, 0, :], gl[:, 0, :], 1.0, None, ALU.add).then_inc(route.sem, 1)
                dve.wait_ge(route.sem, route.at(t, "plus1"))
                dve.reciprocal(shared[:, 0, :], shared[:, 0, :]).then_inc(route.sem, 1)
                dve.reciprocal(gl[:, 1, :], gl[:, 0, :]).then_inc(route.sem, 1)
                dve.wait_ge(route.sem, route.at(t, "inverse"))
                dve.tensor_tensor(shared[:, 0, :], psC[:, 0, 0:P], shared[:, 0, :], ALU.mult).then_inc(route.sem, 1)
                dve.tensor_tensor(gl[:, 2, :], gl[:, 1, :], gate_bias[:], ALU.add).then_inc(route.sem, 1)
                dve.wait_ge(route.sem, route.at(t, "scores"))
                dve.tensor_tensor(shared[:, 1, :], psC[:, 0, P:2 * P], shared[:, 0, :], ALU.mult).then_inc(route.sem, 1)
                dve.max(top[:], gl[:, 2, :]).then_inc(route.sem, 1)

            def m_g2(t):
                dve.wait_ge(route.sem, route.at(t, "top"))
                carry()
                dve.max_index(topi[:], top[:], gl[:, 2, :]).then_inc(route.sem, 1)
                dve.wait_ge(route.sem, route.at(t, "index"))
                dve.tensor_copy(topf[:], topi[:]).then_inc(route.sem, 1)
                dve.wait_ge(route.sem, route.at(t, "index_f"))
                for k in range(TOPK):
                    dve.tensor_scalar(hot[:, k, :], expert_no[:], topf[:, k:k + 1], None, ALU.is_equal).then_inc(route.sem, 1)

            def m_g3(t):
                dve.wait_ge(route.sem, route.at(t, "hot"))
                with nc.allow_low_precision(reason="0 and 1 are exact"):
                    dve.tensor_reduce(sel[:], hot[:].rearrange("p k e -> p e k"), AX.X, ALU.add).then_inc(route.sem, 1)
                dve.tensor_tensor(hot2[:], hot[:], gl[:, 1, :].unsqueeze(1).broadcast_to([P, TOPK, E]), ALU.mult).then_inc(route.sem, 1)
                dve.wait_ge(route.sem, route.at(t, "chosen"))
                dve.tensor_reduce(rt[:, 0, :], hot2[:], AX.X, ALU.add).then_inc(route.sem, 1)
                dve.wait_ge(route.sem, route.at(t, "weight"))
                dve.tensor_reduce(rt[:, 1, 0:1], rt[:, 0, :], AX.X, ALU.add).then_inc(route.sem, 1)
                dve.wait_ge(route.sem, route.at(t, "total"))
                dve.tensor_scalar(rt[:, 1, 1:2], rt[:, 1, 0:1], 1e-12, None, ALU.max).then_inc(route.sem, 1)
                dve.wait_ge(route.sem, route.at(t, "guarded"))
                dve.reciprocal(rt[:, 1, 2:3], rt[:, 1, 1:2]).then_inc(route.sem, 1)
                dve.wait_ge(route.sem, route.at(t, "over_total"))
                dve.tensor_scalar(rt[:, 2, :], rt[:, 0, :], rt[:, 1, 2:3], None, ALU.mult).then_inc(route.sem, 1)

            def m_out(t):
                p = t.par
                dve.wait_ge(route.sem, route.at(t, "pos_ps"))
                dve.tensor_tensor(hot2[:], hot[:], psC[:, 1, 0:E].unsqueeze(1).broadcast_to([P, TOPK, E]), ALU.mult).then_inc(route.sem, 1)
                dve.tensor_tensor(part[:, p, :], psC[:, 0, 0:D], xc_of(t), ALU.add).then_inc(route.sem, 1)
                dve.wait_ge(route.sem, route.at(t, "hot_pos"))
                dve.tensor_reduce(rt[:, 3, :], hot2[:], AX.X, ALU.add).then_inc(route.sem, 1)

            def m_put(t):
                p = t.par
                dve.wait_ge(route.sem, route.at(t, "pos"))
                dve.tensor_tensor(seen[:], seen[:], sel[:], ALU.add).then_inc(route.sem, 1)
                dve.tensor_scalar(rt[:, 4, :], rt[:, 3, :], float(CAP), None, ALU.is_lt).then_inc(route.sem, 1)
                dve.tensor_scalar(rt[:, 5, :], rt[:, 3, :], float(CAP), FAR, ALU.is_ge, ALU.mult).then_inc(route.sem, 1)
                dve.tensor_scalar(rt[:, 6, :], topf[:, 0:TOPK], float(CAP), None, ALU.mult).then_inc(route.sem, 1)
                dve.tensor_scalar(row_meta[:, p, :, 0], topf[:, 0:TOPK], 0.0, token[:, 0:1], ALU.mult, ALU.add).then_inc(route.sem, 1)
                dve.wait_ge(route.sem, route.at(t, "limits"))
                dve.tensor_tensor(row_meta[:, p, :, 1].bitcast(F32), rt[:, 2, :], rt[:, 4, :], ALU.mult).then_inc(route.sem, 1)
                dve.tensor_tensor(rt[:, 7, :], rt[:, 6, :], rt[:, 5, :], ALU.add).then_inc(route.sem, 1)
                dve.tensor_scalar(token[:], token[:], float(P), None, ALU.add).then_inc(route.sem, 1)
                dve.wait_ge(route.sem, route.at(t, "places"))
                dve.tensor_tensor(put[:, p, :], rt[:, 7, :], rt[:, 3, :], ALU.add).then_inc(route.sem, 1)

            run(dve, {k: v for k, v in locals().items() if k in STAGE_NAMES})

            def expert_up(e):
                p = e.par
                dve.wait_ge(ex_exp.sem, ex_exp.at(e, 0))
                h = ex_h[:, p]
                dve.tensor_scalar(h[:, 0, :], h[:, 0, :], 1.0, None, ALU.add).then_inc(ex_act.sem, 1)
                dve.wait_ge(ex_act.sem, ex_act.at(e, "plus1"))
                dve.reciprocal(h[:, 0, :], h[:, 0, :]).then_inc(ex_act.sem, 1)
                dve.wait_ge(ex_act.sem, ex_act.at(e, "inverse"))
                dve.tensor_tensor(h[:, 0, :], psS[p][:, 0:CAP], h[:, 0, :], ALU.mult).then_inc(ex_act.sem, 1)
                dve.wait_ge(ex_act.sem, ex_act.at(e, "silu"))
                dve.tensor_tensor(h[:, 1, :], psS[p][:, CAP:2 * CAP], h[:, 0, :], ALU.mult).then_inc(ex_act.sem, 1)

            skewed(dve, (expert_up, 1))


_T = ["L0_xattn_Wk", "L0_ffn_w1", "L0_ffn_w2", "L1_xattn_Wo", "L1_ffn_gate_w", "L1_ffn_sw1", "L1_ffn_sw3", "L1_ffn_sw2"]


def constants(tokens):
    p = np.arange(P)
    f = np.float32
    c = {"c_ident": np.eye(P, dtype=f),
         "c_head_mask": ((p[:, None] % S) // HD == np.arange(4)[None, :]).astype(f),
         "c_before": (p[:, None] < p[None, :]).astype(f),
         "c_expert_no": np.tile(np.arange(E, dtype=f), (P, 1))}
    inv_freq = f(1.0) / np.power(f(10000.0), np.arange(0, HD, 2, dtype=f) / f(HD))
    ang = (p % S).astype(f)[:, None] * inv_freq[None, :]
    sin, cos = np.sin(ang), np.cos(ang)
    c["c_rope_cos"] = np.tile(np.concatenate([cos, cos], 1), (1, 2 * H)).astype(f)
    c["c_rope_sin"] = np.tile(np.concatenate([-sin, sin], 1), (1, 2 * H)).astype(f)
    slopes = f(1.0) / np.power(f(2.0), np.arange(H, dtype=f) / f(H))
    g, cc, s = np.meshgrid(np.arange(2), np.arange(2), np.arange(2), indexing="ij")
    head = 2 * (4 * cc + 2 * g + s).reshape(-1)[None, :] + (p // S)[:, None]
    rel = np.arange(S, dtype=f)[None, :] - (p % S).astype(f)[:, None]
    c["c_token"] = p.astype(f)[:, None]
    c["c_zero_rows"] = np.zeros((CAP, D), f)
    c["c_places"] = np.stack([tokens + np.arange(E * CAP) % CAP, np.zeros(E * CAP)], 1).astype(np.int32)
    c["c_alibi"] = (slopes[head][:, :, None] * rel[:, None, :]).reshape(P, -1).astype(f)
    return c


def kernel(**inputs):
    import concourse.bacc as bacc
    from concourse.bass_utils import run_bass_kernel_spmd

    arrays = {}
    for name, v in inputs.items():
        v = np.asarray(v)
        if name == "x":
            v = v.reshape(-1, D)
        elif name == "ctx_1024":
            arrays["ctx"] = np.ascontiguousarray(v)
            arrays["ctxT"] = np.ascontiguousarray(v.transpose(0, 2, 1))
            continue
        elif name == "mask_Bx1xSxS2_ik1":
            name, v = "mask", v[:, 0]
        elif name in _T:
            name, v = name + "T", v.T
        elif name in ("L1_ffn_W1", "L1_ffn_W3", "L1_ffn_W2"):
            v = v.reshape(-1, v.shape[-1])
        elif name in ("L1_attn_bq", "L1_attn_bk"):
            v = v.reshape(DC, P).T
        arrays[name] = np.ascontiguousarray(v)
    arrays.update(constants(arrays["x"].shape[0]))

    nc = bacc.Bacc("TRN2", target_bir_lowering=False, num_devices=1)
    a = {n: nc.dram_tensor("in_" + n, v.shape, mybir.dt.from_np(v.dtype), kind="ExternalInput").ap()
         for n, v in arrays.items()}
    a["out"] = nc.dram_tensor("out_x", (arrays["x"].shape[0] + CAP, D), F32, kind="ExternalOutput").ap()
    build(nc, a)
    r = run_bass_kernel_spmd(nc, [{"in_" + n: v for n, v in arrays.items()}], core_ids=[0])
    return np.asarray(r.results[0]["out_x"])[:arrays["x"].shape[0]].reshape(np.shape(inputs["x"]))
```
